# Optimizing a Trainium2 kernel written in Bass

```python
import numpy as np
import jax
import jax.numpy as jnp

def _softmax(x, axis=-1):
    return jax.nn.softmax(x, axis=axis)

def _gelu(x):
    return jax.nn.gelu(x, approximate=True)

def _silu(x):
    return jax.nn.silu(x)

def _sigmoid(x):
    return jax.nn.sigmoid(x)

def _layernorm(x, axis=-1, eps=1e-05):
    m = jnp.mean(x, axis=axis, keepdims=True)
    v = jnp.var(x, axis=axis, keepdims=True)
    return (x - m) / jnp.sqrt(v + eps)

def _scatter_add(tgt, idx, src, axis=0):
    return tgt.at[idx].add(src)

def _segment_sum(src, seg, n):
    return jax.ops.segment_sum(src, seg, n)
kernel_name = 'mk_gnn_preln_d1_gnn_r8_ab0a2d'

def setup_inputs(seed: int=0):
    np.random.seed(seed)
    _w = jnp.asarray

    def _rec_inputs():
        import jax
        import jax.numpy as jnp
        _gk = jax.random.key(seed)
        x = -0.0003713 + 1 * jax.random.normal(jax.random.fold_in(_gk, 1), (6250, 256), jnp.float32)
        _s = jax.random.randint(jax.random.fold_in(_gk, 2), (50000,), 0, 6250, jnp.int32)
        _d = jax.random.randint(jax.random.fold_in(_gk, 3), (50000,), 0, 6250, jnp.int32)
        _loop = jnp.arange(6250, dtype=jnp.int32)
        src = jnp.concatenate([_s, _d, _loop])
        dst = jnp.concatenate([_d, _s, _loop])
        _o = jnp.argsort(dst, stable=True)
        src = src[_o]
        dst = dst[_o]
        edge_attr_32 = -5.3897e-05 + 0.999841 * jax.random.normal(jax.random.fold_in(_gk, 11), (106250, 32), jnp.float32)
        return (x, src, dst, edge_attr_32)
    x, src, dst, edge_attr_32 = _rec_inputs()

    def _L0_gnn_setup():
        import jax, jax.numpy as jnp
        import numpy as np
        N, E = (6250, 100000)
        H, F, R = (256, 128, 32)
        EPS = 1e-05

        def layernorm(x, g, b):
            mu = jnp.mean(x, axis=-1, keepdims=True)
            var = jnp.mean(jnp.square(x - mu), axis=-1, keepdims=True)
            return (x - mu) * jax.lax.rsqrt(var + EPS) * g + b
        key = jax.random.key(seed)
        ks = jax.random.split(key, 12)
        s = 0.02
        return {'x': jax.random.normal(ks[0], (N, H), jnp.float32), 'rbf': jax.random.normal(ks[1], (E, R), jnp.float32), 'edge_index': jax.random.randint(ks[2], (2, E), 0, N, jnp.int32), 'ntm_w': jax.random.normal(ks[3], (F, H), jnp.float32) * s, 'ntm_b': jnp.zeros((F,), jnp.float32), 'rtm_w': jax.random.normal(ks[4], (F, R), jnp.float32) * s, 'rtm_b': jnp.zeros((F,), jnp.float32), 'norm_g': jnp.ones((F,), jnp.float32), 'norm_b': jnp.zeros((F,), jnp.float32), 'l1_w': jax.random.normal(ks[5], (F, 3 * F), jnp.float32) * s, 'l1_b': jnp.zeros((F,), jnp.float32), 'ln_g': jnp.ones((F,), jnp.float32), 'ln_b': jnp.zeros((F,), jnp.float32), 'l2_w': jax.random.normal(ks[6], (F, F), jnp.float32) * s, 'l2_b': jnp.zeros((F,), jnp.float32), 'mtn_w': jax.random.normal(ks[7], (H, F), jnp.float32) * s}
    _L0_gnn_all = _L0_gnn_setup()
    _L0_gnn_in = {k: v for k, v in _L0_gnn_all.items() if k in ('ntm_w', 'ntm_b', 'rtm_w', 'rtm_b', 'norm_g', 'norm_b', 'l1_w', 'l1_b', 'ln_g', 'ln_b', 'l2_w', 'l2_b', 'mtn_w')}
    del _L0_gnn_all
    return {'x': x, 'src': src, 'dst': dst, 'edge_attr_32': edge_attr_32, 'L0_gnn_ntm_w': _L0_gnn_in['ntm_w'], 'L0_gnn_ntm_b': _L0_gnn_in['ntm_b'], 'L0_gnn_rtm_w': _L0_gnn_in['rtm_w'], 'L0_gnn_rtm_b': _L0_gnn_in['rtm_b'], 'L0_gnn_norm_g': _L0_gnn_in['norm_g'], 'L0_gnn_norm_b': _L0_gnn_in['norm_b'], 'L0_gnn_l1_w': _L0_gnn_in['l1_w'], 'L0_gnn_l1_b': _L0_gnn_in['l1_b'], 'L0_gnn_ln_g': _L0_gnn_in['ln_g'], 'L0_gnn_ln_b': _L0_gnn_in['ln_b'], 'L0_gnn_l2_w': _L0_gnn_in['l2_w'], 'L0_gnn_l2_b': _L0_gnn_in['l2_b'], 'L0_gnn_mtn_w': _L0_gnn_in['mtn_w']}

def reference(x, src, dst, edge_attr_32, L0_gnn_ntm_w, L0_gnn_ntm_b, L0_gnn_rtm_w, L0_gnn_rtm_b, L0_gnn_norm_g, L0_gnn_norm_b, L0_gnn_l1_w, L0_gnn_l1_b, L0_gnn_ln_g, L0_gnn_ln_b, L0_gnn_l2_w, L0_gnn_l2_b, L0_gnn_mtn_w):
    import jax
    import jax.numpy as jnp

    def _L0_gnn_ref(x, rbf, edge_index, ntm_w, ntm_b, rtm_w, rtm_b, norm_g, norm_b, l1_w, l1_b, ln_g, ln_b, l2_w, l2_b, mtn_w):
        import jax, jax.numpy as jnp
        import numpy as np
        N, E = (6250, 100000)
        H, F, R = (256, 128, 32)
        EPS = 1e-05

        def layernorm(x, g, b):
            mu = jnp.mean(x, axis=-1, keepdims=True)
            var = jnp.mean(jnp.square(x - mu), axis=-1, keepdims=True)
            return (x - mu) * jax.lax.rsqrt(var + EPS) * g + b
        edge_attr = rbf @ rtm_w.T + rtm_b
        xf = layernorm(x @ ntm_w.T + ntm_b, norm_g, norm_b)
        i, j = (edge_index[0], edge_index[1])
        cat = jnp.concatenate((xf[i], xf[j], edge_attr), axis=-1)
        h = layernorm(cat @ l1_w.T + l1_b, ln_g, ln_b)
        m = jax.nn.gelu(h, approximate=False) @ l2_w.T + l2_b
        agg = jax.ops.segment_sum(m, j, num_segments=x.shape[0])
        return agg @ mtn_w.T
    edge_index = jnp.stack([src, dst])
    h = jnp.maximum(_layernorm(x, axis=-1), 0.0)
    x = x + _L0_gnn_ref(h, edge_attr_32, edge_index, L0_gnn_ntm_w, L0_gnn_ntm_b, L0_gnn_rtm_w, L0_gnn_rtm_b, L0_gnn_norm_g, L0_gnn_norm_b, L0_gnn_l1_w, L0_gnn_l1_b, L0_gnn_ln_g, L0_gnn_ln_b, L0_gnn_l2_w, L0_gnn_l2_b, L0_gnn_mtn_w)
    return x

_drawn_inputs = setup_inputs


def setup_inputs(seed=0):
    import zlib

    import numpy as np

    out = dict(_drawn_inputs(seed))
    spreads = {'L0_gnn_ntm_b': (0.0, 0.1),
     'L0_gnn_rtm_b': (0.0, 1.166),
     'L0_gnn_norm_g': (1.0, 0.6),
     'L0_gnn_norm_b': (0.0, 0.563),
     'L0_gnn_l1_b': (0.0, 0.289),
     'L0_gnn_ln_g': (1.0, 0.2),
     'L0_gnn_ln_b': (0.0, 0.1),
     'L0_gnn_l2_b': (0.0, 0.1)}
    factors = {'edge_attr_32': 6.675, 'L0_gnn_rtm_w': 6.715}
    for name, (base, spread) in spreads.items():
        noise = np.random.default_rng([zlib.crc32(name.encode()), seed]).standard_normal(out[name].shape)
        drawn = base * np.exp(spread * noise) if base else spread * noise
        out[name] = jnp.asarray(drawn.astype(out[name].dtype))
    for name, factor in factors.items():
        out[name] = (out[name] * factor).astype(out[name].dtype)
    return out
```

```python
from contextlib import ExitStack

import concourse.bass as bass
from concourse import mybir

ALU = mybir.AluOpType
ACT = mybir.ActivationFunctionType
F32 = mybir.dt.float32
BF16 = mybir.dt.bfloat16
I32 = mybir.dt.int32
U32 = mybir.dt.uint32

P = 128
EPS = 1e-5
NODES, HID, FEAT, RBF = 6250, 256, 128, 32
EDGES = 106250

CT = 4
CHUNK = CT * P
FULL_CHUNKS = NODES // CHUNK
LAST_ROWS = NODES - FULL_CHUNKS * CHUNK
CHUNKS = FULL_CHUNKS + 1
NODE_TILES = FULL_CHUNKS * CT + 1
assert 0 < LAST_ROWS <= P

GT = 8
GROUP = GT * P
PAIRS = -(-EDGES // (2 * GROUP))
GROUPS = 2 * PAIRS
EDGE_TILES = GROUPS * GT
PAD_EDGES = EDGE_TILES * P
HEAD_PAIRS, TAIL_PAIRS = 2, 2
assert (PAIRS - HEAD_PAIRS - TAIL_PAIRS) % 2 == 0

WIN = 80
RBF_ROW = 96
TABLE_ROWS = 6400
WINDOWS = -(-NODES // WIN)
assert NODES + WIN <= TABLE_ROWS and WINDOWS * WIN <= TABLE_ROWS

RSQRT_MAGIC = 0x5F3759DF
NT_STEPS = 12
N_CONSTS = 10
N_WEIGHTS = 18
N_IDX = 6
ENGINES = 5
HANDLED = -1.0e6


def bass_gnn_layer(nc, x, src, dst, rbf_t, ntm_w, ntm_b, rtm_w, rtm_b, norm_g, norm_b,
                   l1_w, l1_b, ln_g, ln_b, l2_w, l2_b, mtn_w, out):
    with ExitStack() as ctx:
        def sb(name, shape, dt=F32):
            return ctx.enter_context(nc.sbuf_tensor(name, shape, dt))

        def psum(name, shape):
            return ctx.enter_context(nc.psum_tensor(name, shape, F32))

        def sem(name):
            return ctx.enter_context(nc.semaphore(name))

        p_table = nc.dram_tensor("p_table", [NODES, FEAT], F32, kind="Internal").ap()
        q_table = nc.dram_tensor("q_table", [TABLE_ROWS, FEAT], F32, kind="Internal").ap()

        ident = sb("ident", [P, P])
        ident_bf = sb("ident_bf", [P, P], BF16)
        center = sb("center", [P, P])
        ones = sb("ones", [P, P])
        ones_bf = sb("ones_bf", [P, P], BF16)
        iota = sb("iota", [P, WIN])
        ntm_s = sb("ntm_s", [FEAT, HID])
        l1_s = sb("l1_s", [FEAT, 3 * FEAT])
        rtm_s = sb("rtm_s", [FEAT, P])
        l2_s = sb("l2_s", [FEAT, FEAT])
        mtn_s = sb("mtn_s", [P, 2, FEAT])
        cols = sb("cols", [P, 8])
        lng_b = sb("lng_b", [P, FEAT])
        lnb_b = sb("lnb_b", [P, FEAT])
        ntm_t = sb("ntm_t", [P, 2, FEAT])
        l1_t = sb("l1_t", [P, 3, FEAT])
        ab_t = sb("ab_t", [P, 2 * FEAT])
        vec_rep = sb("vec_rep", [P, 3, P])
        q_bias = sb("q_bias", [P, FEAT])
        ntm_bc = sb("ntm_bc", [P, 1])
        mtn_t = sb("mtn_t", [P, HID])
        l2_t = sb("l2_t", [P, FEAT])
        l2b_row = sb("l2b_row", [1, FEAT])

        x_s = sb("x_s", [P, NODE_TILES, HID])
        bn6 = sb("bn6", [P, 2, CT, 6])
        mv = sb("mv", [P, 2, CT, 2])
        rs = sb("rs", [P, 2, 6, CT])
        rs2 = sb("rs2", [P, 2, 5, CT])
        pq_s = sb("pq_s", [P, 2, CT, 2 * FEAT])

        src_s = sb("src_s", [P, 2, 2 * GT], I32)
        dst_i = sb("dst_i", [P, EDGE_TILES], I32)
        dst_f = sb("dst_f", [P, EDGE_TILES])
        rel = sb("rel", [P, EDGE_TILES])
        miss = sb("miss", [P, EDGE_TILES])
        miss_n = sb("miss_n", [P, 2])
        base = sb("base", [1, GROUPS], I32)
        miss_i = sb("miss_i", [1, 1], I32)
        acc = sb("acc", [P, 2, TABLE_ROWS])
        gath = sb("gath", [P, 2, 2, GT, FEAT])
        onehot = sb("onehot", [P, 4, GT, WIN])
        edge_t = sb("edge_t", [P, 2, GROUP])
        win_q = sb("win_q", [P, 2, FEAT])
        z = sb("z", [P, 2, 2, GT, FEAT])
        ssum = sb("ssum", [P, 2, 2 * GT])
        nt = sb("nt", [P, 3, 2 * GT])
        gel = sb("gel", [P, 2, GT, FEAT])
        h_s = z[:, 0, :, :, :].rearrange("p s t f -> p s (t f)").rearrange("p s (t h) -> p s t h", t=CT)
        ht_s = z[:, 1, :, :, :].rearrange("p s t f -> p s (t f)").rearrange("p s (k n) -> p s k n", k=2)
        yc_s = gath[:, 1, 0, :, :].rearrange("p t f -> p (t f)").rearrange("p (s n) -> p s n", s=2)
        ysq_s = gath[:, 1, 1, :, :].rearrange("p t f -> p (t f)").rearrange("p (s n) -> p s n", s=2)
        msg_s = gath[:, 0, 0, :, :].rearrange("p t f -> p (t f)").rearrange("p (s n) -> p s n", s=2)
        fin = gel[:, :, :, :].rearrange("p s t f -> p s (t f)").rearrange("p s (t h) -> p s t h", t=CT)

        pre_ps = psum("pre_ps", [P, 2, GROUP])
        oht_ps = psum("oht_ps", [P, GROUP])
        agg_ps = psum("agg_ps", [P, 2, 512])
        pq_ps = pre_ps[:, 0, :].rearrange("p (k t f) -> p k t f", k=2, t=CT)
        y_ps = pre_ps[:, 1, :].rearrange("p (s n) -> p s n", s=2)
        ht_ps = oht_ps[:, :].rearrange("p (k n) -> p k n", k=2)
        ss_ps = agg_ps[:, 0, :]
        set_ps = agg_ps[:, 1, :]

        w_in = sem("w_in")
        bc_in = sem("bc_in")
        idx_in = sem("idx_in")
        consts = sem("consts")
        w_mm = sem("w_mm")
        w_done = sem("w_done")
        idx_done = sem("idx_done")
        acc_zero = sem("acc_zero")
        zero_out = sem("zero_out")
        x_in = [sem("x_in0"), sem("x_in1")]
        bn_step = sem("bn_step")
        aggr_turn = sem("aggr_turn")
        var_ready = sem("var_ready")
        sd_ready = sem("sd_ready")
        r_step = sem("r_step")
        norm_ready = sem("norm_ready")
        h_ready = sem("h_ready")
        ht_ready = sem("ht_ready")
        ht_copied = sem("ht_copied")
        y_ready = sem("y_ready")
        yc_ready = sem("yc_ready")
        pq_ready = sem("pq_ready")
        ssv_ready = sem("ssv_ready")
        sd2_ready = sem("sd2_ready")
        r2_step = sem("r2_step")
        r2_ready = sem("r2_ready")
        p_scaled = sem("p_scaled")
        q_scaled = sem("q_scaled")
        p_out = [sem("p_out0"), sem("p_out1")]
        q_out = [sem("q_out0"), sem("q_out1")]
        s_ready = sem("s_ready")
        oht_ready = sem("oht_ready")
        oht_copied = sem("oht_copied")
        src_in = [sem("src_in0"), sem("src_in1")]
        rbf_in = [sem("rbf_in0"), sem("rbf_in1")]
        q_in = [sem("q_in0"), sem("q_in1")]
        pre_ready = sem("pre_ready")
        gathered = [[[sem(f"gathered{s}{h}{a}") for a in range(2)] for h in range(2)] for s in range(2)]
        gather_turn = sem("gather_turn")
        sum_ready = sem("sum_ready")
        ssum_ready = sem("ssum_ready")
        nt_step = sem("nt_step")
        norm_step = sem("norm_step")
        z_ready = sem("z_ready")
        gelu_ready = sem("gelu_ready")
        agg_ready = sem("agg_ready")
        agg_added = sem("agg_added")
        pass_sems = [s_ready, oht_ready, oht_copied, *src_in, *rbf_in, *q_in, pre_ready,
                     *(s for a in gathered for b in a for s in b),
                     gather_turn, sum_ready, ssum_ready, nt_step, norm_step, z_ready, gelu_ready, agg_ready,
                     agg_added]
        pass_end = sem("pass_end")
        windows_set = sem("windows_set")
        win_step = sem("win_step")
        clear_turn = sem("clear_turn")
        out_ready = sem("out_ready")
        msg_ready = sem("msg_ready")
        msg_copied = sem("msg_copied")
        fin_ready = sem("fin_ready")
        o_out = [sem("o_out0"), sem("o_out1")]

        def slot_loaded(n, slot):
            return 16 * ((n - slot) // 2 + 1) if isinstance(n, int) else 8 * (n - slot) + 16

        def over_pairs(eng, pair):
            for p in range(HEAD_PAIRS):
                pair(p, p % 2, p == 0, False, False)
            with eng.Fori(0, (PAIRS - HEAD_PAIRS - TAIL_PAIRS) // 2) as i:
                for j in range(2):
                    pair(2 * i + (HEAD_PAIRS + j), j, False, True, False)
            for p in range(PAIRS - TAIL_PAIRS, PAIRS):
                pair(p, p % 2, False, True, p == PAIRS - 1)

        def pass_sync(sp):
            def loads(g, h, warm):
                start = sp.value_load(base[0:1, bass.ds(g, 1)], min_val=0, max_val=NODES)
                if warm:
                    sp.wait_ge(pre_ready, g - 1)
                sp.dma_start(edge_t[RBF_ROW:P, h, :], rbf_t[:, bass.ds(g * GROUP, GROUP)])\
                  .then_inc(rbf_in[h], 16)
                sp.dma_start(win_q[0:WIN, h, :], q_table[bass.ds(start, WIN), :])\
                  .then_inc(q_in[h], 16)

            def sources(p, par):
                sp.dma_start(src_s[:, par, :], src[bass.ds(p, 1), :, :].rearrange("a p t -> (a p) t"))\
                  .then_inc(src_in[par], 16)

            def pair(p, par, first, warm, last):
                for h in range(2):
                    loads(2 * p + h, h, not first)
                if not last:
                    if not first:
                        sp.wait_ge(sum_ready, 4 * p)
                    sources(p + 1, 1 - par)

            sources(0, 0)
            over_pairs(sp, pair)

        def pass_gpsimd(pool):
            def pair(p, par, first, warm, last):
                pool.wait_ge(src_in[par], slot_loaded(p, par))
                for h in range(2):
                    g = 2 * p + h
                    if warm:
                        pool.wait_ge(sum_ready, 2 * g - 6)
                    pool.sem_inc(gather_turn, 1)
                    for t in range(GT):
                        pool.indirect_dma_start(
                            out=gath[:, par, h, t, :], out_offset=None, in_=p_table,
                            in_offset=bass.IndirectOffsetOnAxis(
                                ap=src_s[:, par, h * GT + t:h * GT + t + 1].bitcast(U32), axis=0),
                        ).then_inc(gathered[par][h][t // (GT // 2)], 16)
            over_pairs(pool, pair)

        HALF = GT // 2

        def pass_vector(dve):
            def one_hot(g, slot, reused):
                if reused:
                    dve.wait_ge(agg_ready, g - 3)
                nc.vector.tensor_tensor(
                    onehot[:, slot, :, :],
                    iota[:, :].unsqueeze(1).to_broadcast([P, GT, WIN]),
                    rel[:, bass.ds(g * GT, GT)].unsqueeze(2).to_broadcast([P, GT, WIN]),
                    ALU.is_equal).then_inc(s_ready, 1)

            def add_sums(g, h):
                start = dve.value_load(base[0:1, bass.ds(g, 1)], min_val=0, max_val=NODES)
                dve.wait_ge(agg_ready, g + 1)
                if not (isinstance(g, int) and g == 0):
                    dve.wait_ge(agg_added, g)
                nc.vector.tensor_tensor(
                    acc[:, :, bass.ds(start, WIN)], acc[:, :, bass.ds(start, WIN)],
                    agg_ps[:, h, 0:2 * WIN].rearrange("p (a w) -> p a w", a=2),
                    ALU.add).then_inc(agg_added, 1)

            def pair(p, par, first, warm, last):
                for h in range(2):
                    g = 2 * p + h
                    dve.wait_ge(pre_ready, g + 1)
                    if warm:
                        dve.wait_ge(gelu_ready, 2 * g - 6)
                    for a in range(2):
                        t = slice(a * HALF, (a + 1) * HALF)
                        dve.wait_ge(gathered[par][h][a], HALF * slot_loaded(p, par))
                        nc.vector.tensor_tensor(
                            z[:, par, h, t, :],
                            pre_ps[:, h, :].rearrange("p (t f) -> p t f", t=GT)[:, t, :],
                            gath[:, par, h, t, :], ALU.add).then_inc(sum_ready, 1)
                    if not last:
                        one_hot(g + 2, (2 * par + h + 2) % 4, not first)
                if not first:
                    for h in range(2):
                        add_sums(2 * p - 2 + h, h)

                step = [0]

                def then_next(ins):
                    step[0] += 1
                    ins.then_inc(nt_step, 1)
                    dve.wait_ge(nt_step, NT_STEPS * p + step[0])
                var, y, t2 = nt[:, 0, :], nt[:, 1, :], nt[:, 2, :]
                dve.wait_ge(ssum_ready, 2 * p + 2)
                then_next(nc.vector.tensor_scalar(var, ssum[:, par, :], 1.0 / FEAT, EPS, ALU.mult, ALU.add))
                then_next(nc.vector.tensor_scalar(t2.bitcast(I32), var.bitcast(I32), 1, None,
                                                  ALU.logical_shift_right))
                then_next(nc.vector.tensor_scalar(y.bitcast(I32), t2.bitcast(I32), -1.0,
                                                  float(RSQRT_MAGIC), ALU.mult, ALU.add))
                for _ in range(3):
                    then_next(nc.vector.tensor_tensor(t2, y, y, ALU.mult))
                    then_next(nc.vector.scalar_tensor_tensor(t2, t2, -0.5, var, ALU.mult, ALU.mult))
                    then_next(nc.vector.scalar_tensor_tensor(y, t2, 1.5, y, ALU.add, ALU.mult))
                assert step[0] == NT_STEPS

                for h in range(2):
                    for a in range(2):
                        for t in range(a * HALF, (a + 1) * HALF):
                            ins = nc.vector.scalar_tensor_tensor(
                                z[:, par, h, t, :], z[:, par, h, t, :], nt[:, 1, h * GT + t:h * GT + t + 1],
                                lng_b[:, :], ALU.mult, ALU.mult)
                        ins.then_inc(norm_step, 1)
                        dve.wait_ge(norm_step, 4 * p + (2 * h + a + 1))
                        t = slice(a * HALF, (a + 1) * HALF)
                        nc.vector.tensor_tensor(
                            z[:, par, h, t, :], z[:, par, h, t, :],
                            lnb_b[:, :].unsqueeze(1).to_broadcast([P, HALF, FEAT]),
                            ALU.add).then_inc(z_ready, 1)

            one_hot(0, 0, False)
            one_hot(1, 1, False)
            over_pairs(dve, pair)
            for h in range(2):
                add_sums(GROUPS - 2 + h, h)

        def pass_scalar(act):
            def copy_one_hot(g, h, reused):
                act.wait_ge(oht_ready, g + 1)
                if reused:
                    act.wait_ge(pre_ready, g - 1)
                nc.scalar.activation(edge_t[0:WIN, h, :], oht_ps[0:WIN, :], ACT.Copy)\
                  .then_inc(oht_copied, 1)

            def pair(p, par, first, warm, last):
                for h in range(2):
                    g = 2 * p + h
                    if not first:
                        act.wait_ge(agg_ready, g - 1)
                    for t in range(GT):
                        if t % HALF == 0:
                            act.wait_ge(sum_ready, 2 * g + 1 + t // HALF)
                        ins = nc.scalar.activation(gel[:, h, t, :], z[:, par, h, t, :], ACT.Square,
                                                   accum_out=ssum[:, par, h * GT + t:h * GT + t + 1])
                    ins.then_inc(ssum_ready, 1)
                    if not last:
                        copy_one_hot(g + 2, h, True)
                for h in range(2):
                    g = 2 * p + h
                    act.wait_ge(ssum_ready, g + 1)
                    for a in range(2):
                        act.wait_ge(z_ready, 2 * g + 1 + a)
                        t = slice(a * HALF, (a + 1) * HALF)
                        nc.scalar.activation(gel[:, h, t, :], z[:, par, h, t, :], ACT.Gelu)\
                          .then_inc(gelu_ready, 1)

            copy_one_hot(0, 0, False)
            copy_one_hot(1, 1, False)
            over_pairs(act, pair)

        def bf16_view(slot, t):
            return onehot[:, slot, t, :].bitcast(BF16)[:, 1::2]

        def pass_tensor(pe):
            def product(g, h, slot, reused):
                pe.wait_ge(s_ready, g + 1)
                if not (isinstance(g, int) and g == 0):
                    pe.wait_ge(oht_copied, g)
                for t in range(GT):
                    ins = nc.tensor.matmul(oht_ps[0:WIN, t * P:(t + 1) * P], bf16_view(slot, t),
                                           ident_bf[:, :], start=True, stop=True)
                ins.then_inc(oht_ready, 1)
                pe.wait_ge(oht_copied, g + 1)
                pe.wait_ge(rbf_in[h], slot_loaded(g, h))
                pe.wait_ge(q_in[h], slot_loaded(g, h))
                if reused:
                    pe.wait_ge(sum_ready, 2 * g - 2)
                for t in range(GT):
                    ins = nc.tensor.matmul(pre_ps[:, h, t * FEAT:(t + 1) * FEAT],
                                           edge_t[:, h, t * P:(t + 1) * P], win_q[:, h, :],
                                           start=True, stop=True)
                ins.then_inc(pre_ready, 1)

            def sums(g, h, slot, reused):
                if reused:
                    pe.wait_ge(agg_added, g - 1)
                for t in range(GT):
                    if t % HALF == 0:
                        pe.wait_ge(gelu_ready, 2 * g + 1 + t // HALF)
                    nc.tensor.matmul(agg_ps[:, h, 0:WIN], gel[:, h, t, :], onehot[:, slot, t, :],
                                     start=(t == 0), stop=(t == GT - 1), skip_group_check=True)
                    ins = nc.tensor.matmul(agg_ps[:, h, WIN:2 * WIN], ones_bf[:, :], bf16_view(slot, t),
                                           start=False, stop=(t == GT - 1), skip_group_check=True)
                ins.then_inc(agg_ready, 1)

            def pair(p, par, first, warm, last):
                for h in range(2):
                    if not last:
                        product(2 * p + 2 + h, h, (2 * par + h + 2) % 4, True)
                for h in range(2):
                    sums(2 * p + h, h, 2 * par + h, not first)

            product(0, 0, 0, False)
            product(1, 1, 1, False)
            over_pairs(pe, pair)

        def missed_passes(eng, edge_pass):
            eng.wait_ge(idx_done, N_IDX)
            missed = eng.value_load(miss_i[0:1, 0:1], min_val=0, max_val=PAD_EDGES)
            with eng.If(missed > 0):
                eng.drain().then_inc(pass_end, 1)
                with eng.Fori(0, WINDOWS) as r:
                    eng.wait_ge(windows_set, r + 1)
                    edge_pass(eng)
                    eng.drain().then_inc(pass_end, 1)

        def missed_passes_vector(dve):
            dve.wait_ge(idx_done, N_IDX)
            missed = dve.value_load(miss_i[0:1, 0:1], min_val=0, max_val=PAD_EDGES)
            with dve.If(missed > 0):
                dve.drain().then_inc(pass_end, 1)
                dve.wait_ge(pass_end, ENGINES)
                nc.vector.tensor_scalar(miss[:, :], miss[:, :], -HANDLED, HANDLED + WIN, ALU.mult, ALU.add)\
                  .then_inc(win_step, 1)
                nc.vector.memset(base[:, :], -WIN).then_inc(win_step, 1)
                dve.wait_ge(win_step, 2)
                nc.vector.tensor_tensor(rel[:, :], dst_f[:, :], miss[:, :], ALU.add).then_inc(win_step, 1)
                with dve.Fori(0, WINDOWS) as r:
                    dve.wait_ge(pass_end, ENGINES * r + ENGINES)
                    dve.sem_inc(clear_turn, 1)
                    for s in pass_sems:
                        dve.sem_clear(s)
                    dve.wait_ge(win_step, 2 * r + 3)
                    nc.vector.tensor_scalar(rel[:, :], rel[:, :], -float(WIN), None, ALU.add)\
                      .then_inc(win_step, 1)
                    nc.vector.tensor_scalar(base[:, :], base[:, :], float(WIN), None, ALU.add)\
                      .then_inc(win_step, 1)
                    dve.wait_ge(win_step, 2 * r + 5)
                    dve.sem_inc(windows_set, 1)
                    pass_vector(dve)
                    dve.drain().then_inc(pass_end, 1)

        with nc.Block() as block:

            def node_chunks(eng, ahead, chunk):
                def both(c, slot, full_next, full, do_next=True):
                    if do_next:
                        ahead(c + 1, 1 - slot, CT if full_next else 1, P if full_next else LAST_ROWS)
                    chunk(c, slot, CT if full else 1, P if full else LAST_ROWS)
                ahead(0, 0, CT, P)
                both(0, 0, True, True)
                with eng.Fori(0, (FULL_CHUNKS - 2) // 2) as i:
                    for j in range(2):
                        both(2 * i + (1 + j), (1 + j) % 2, True, True)
                both(FULL_CHUNKS - 1, (FULL_CHUNKS - 1) % 2, False, True)
                both(FULL_CHUNKS, FULL_CHUNKS % 2, False, False, do_next=False)

            def nothing(*_):
                pass

            @block.sync
            def _(sp):
                for dram, sbuf in ((ntm_w, ntm_s[:, :]), (l1_w, l1_s[:, :]),
                                   (l2_w, l2_s[:, :]),
                                   (mtn_w.rearrange("(a p) f -> p a f", p=P), mtn_s[:, :, :])):
                    sp.dma_start(sbuf, dram).then_inc(w_in, 16)
                sp.wait_ge(consts, N_CONSTS)
                sp.dma_start(rtm_s[:, RBF_ROW:P], rtm_w).then_inc(w_in, 16)
                sp.dma_start(dst_i[:, :], dst).then_inc(idx_in, 16)
                for c in range(CHUNKS):
                    if c >= 2:
                        sp.wait_ge(x_in[c % 2], 16 * (c // 2))
                    if c < FULL_CHUNKS:
                        sp.dma_start(x_s[:, c * CT:(c + 1) * CT, :],
                                      x[c * CHUNK:(c + 1) * CHUNK, :].rearrange("(t p) h -> p t h", p=P))\
                           .then_inc(x_in[c % 2], 16)
                    else:
                        sp.dma_start(x_s[0:LAST_ROWS, c * CT, :], x[c * CHUNK:NODES, :]).then_inc(x_in[c % 2], 16)
                sp.wait_ge(acc_zero, 1)
                pad_rows = TABLE_ROWS - NODES
                sp.dma_start(q_table[NODES:TABLE_ROWS, :].rearrange("(a b) f -> a (b f)", b=3),
                             acc[0:pad_rows // 3, 0, 0:3 * FEAT]).then_inc(zero_out, 16)

                def store(c, slot, tiles, rows):
                    sp.wait_ge(p_scaled, c + 1)
                    sp.wait_ge(q_scaled, c + 1)
                    for k, (table, done) in enumerate(((p_table, p_out), (q_table, q_out))):
                        part = slice(k * FEAT, (k + 1) * FEAT)
                        if tiles == CT:
                            sp.dma_start(table[bass.ds(c * CHUNK, CHUNK), :].rearrange("(t p) f -> p t f", p=P),
                                         pq_s[:, slot, :, part]).then_inc(done[slot], 16)
                        else:
                            sp.dma_start(table[c * CHUNK:NODES, :], pq_s[0:rows, slot, 0, part])\
                              .then_inc(done[slot], 16)
                node_chunks(sp, nothing, store)
                sp.wait_ge(zero_out, 16)
                for slot in range(2):
                    last = CHUNKS - 1 if (CHUNKS - 1) % 2 == slot else CHUNKS - 2
                    sp.wait_ge(q_out[slot], slot_loaded(last, slot))
                sp.wait_ge(idx_done, N_IDX)
                sp.wait_ge(w_done, N_WEIGHTS)
                pass_sync(sp)
                missed_passes(sp, pass_sync)

            @block.gpsimd
            def _(pool):
                def then_const(ins):
                    ins.then_inc(consts, 1)
                then_const(nc.gpsimd.memset(ident[:, :], 0.0))
                then_const(nc.gpsimd.memset(center[:, :], -1.0 / FEAT))
                then_const(nc.gpsimd.memset(rtm_s[:, :], 0.0))
                then_const(nc.gpsimd.memset(ones[:, :], 1.0))
                then_const(nc.gpsimd.memset(ones_bf[:, :], 1.0))
                then_const(nc.gpsimd.iota(iota[:, :], [[1, WIN]], base=0, channel_multiplier=0,
                                          allow_small_or_imprecise_dtypes=True))
                pool.wait_ge(consts, 6)
                then_const(nc.gpsimd.affine_select(out=ident[:, :], in_=ident[:, :], compare_op=ALU.not_equal,
                                                   fill=1.0, base=0, pattern=[[-1, P]], channel_multiplier=1))
                then_const(nc.gpsimd.affine_select(out=center[:, :], in_=center[:, :], compare_op=ALU.not_equal,
                                                   fill=1.0 - 1.0 / FEAT, base=0, pattern=[[-1, P]],
                                                   channel_multiplier=1))
                pool.wait_ge(consts, 8)
                then_const(nc.gpsimd.tensor_copy(ident_bf[:, :], ident[:, :]))
                then_const(nc.gpsimd.memset(edge_t[:, :, :], 0.0))
                nc.gpsimd.memset(acc[:, :, :], 0.0).then_inc(acc_zero, 1)
                for slot in range(2):
                    last = CHUNKS - 1 if (CHUNKS - 1) % 2 == slot else CHUNKS - 2
                    pool.wait_ge(p_out[slot], slot_loaded(last, slot))
                pass_gpsimd(pool)
                missed_passes(pool, pass_gpsimd)

            @block.tensor
            def _(pe):
                pe.wait_ge(w_in, 16 * 5)
                pe.wait_ge(consts, N_CONSTS)
                products = [(ntm_s[:, 0:P], center[:, :]), (ntm_s[:, P:HID], center[:, :]),
                            (l1_s[:, 0:P], center[:, :]), (l1_s[:, P:2 * P], center[:, :]),
                            (l1_s[:, 2 * P:3 * P], center[:, :])]
                done = 1
                for lhs, rhs in products:
                    pe.wait_ge(w_done, done)
                    nc.tensor.matmul(set_ps[:, 0:P], lhs, rhs, start=True, stop=True).then_inc(w_mm, 1)
                    done += 1
                pe.wait_ge(w_done, 11)
                for n, (lhs, rhs) in enumerate(((vec_rep[:, 0, :], l1_t[:, 0, :]), (vec_rep[:, 0, :], l1_t[:, 1, :]),
                                                (vec_rep[:, 1, :], l1_t[:, 2, :]), (vec_rep[:, 2, :], center[:, :]))):
                    ins = nc.tensor.matmul(set_ps[:, 0:P], lhs, rhs, start=(n == 0), stop=(n == 3))
                ins.then_inc(w_mm, 1)
                pe.wait_ge(w_done, 12)
                nc.tensor.matmul(set_ps[:, 0:P], rtm_s[:, :], l1_t[:, 2, :], start=True, stop=True).then_inc(w_mm, 1)
                pe.wait_ge(w_done, 14)
                nc.tensor.matmul(set_ps[:, 0:1], center[:, :], cols[:, 0:1], start=True, stop=True).then_inc(w_mm, 1)
                for a, w in enumerate((mtn_s[:, 0, :], mtn_s[:, 1, :], l2_s[:, :])):
                    pe.wait_ge(w_done, 15 + a)
                    nc.tensor.transpose(set_ps[:, 0:P], w, ident[:, :]).then_inc(w_mm, 1)
                pe.wait_ge(w_done, N_WEIGHTS)
                pe.wait_ge(idx_done, 1)
                nc.tensor.matmul(set_ps[:, 0:GROUPS], ones[0:1, :], dst_f[0:1, ::GT], start=True, stop=True)\
                  .then_inc(w_mm, 1)
                pe.wait_ge(idx_done, 5)
                nc.tensor.matmul(set_ps[0:1, 0:2], miss_n[:, 0:1], ones[:, 0:2], start=True, stop=True)\
                  .then_inc(w_mm, 1)

                def chunk(c, slot, tiles, rows):
                    n = (tiles - 1) * P + rows
                    pe.wait_ge(h_ready, c + 1)
                    if not (isinstance(c, int) and c == 0):
                        pe.wait_ge(ht_copied, c)
                    for t in range(tiles):
                        for k in range(2):
                            ins = nc.tensor.transpose(ht_ps[:, k, t * P:t * P + rows],
                                                      h_s[0:rows, slot, t, k * P:(k + 1) * P],
                                                      ident[0:rows, 0:rows])
                    ins.then_inc(ht_ready, 1)
                    pe.wait_ge(ht_copied, c + 1)
                    if not (isinstance(c, int) and c < 2):
                        pe.wait_ge(yc_ready, 2 * c - 2)
                    for k in range(2):
                        ins = nc.tensor.matmul(y_ps[:, slot, 0:n], ntm_t[:, k, :], ht_s[:, slot, k, 0:n],
                                               start=(k == 0), stop=(k == 1))
                    ins.then_inc(y_ready, 1)
                    pe.wait_ge(yc_ready, 2 * c + 2)
                    if not (isinstance(c, int) and c == 0):
                        pe.wait_ge(ssv_ready, c)
                        pe.wait_ge(p_scaled, c)
                        pe.wait_ge(q_scaled, c)
                    for t in range(tiles):
                        nc.tensor.matmul(ss_ps[0:rows, t:t + 1], ysq_s[:, slot, t * P:t * P + rows],
                                         ones[:, 0:1], start=True, stop=True)
                    for t in range(tiles):
                        for k in range(2):
                            ins = nc.tensor.matmul(pq_ps[0:rows, k, t, :], yc_s[:, slot, t * P:t * P + rows],
                                                   ab_t[:, k * FEAT:(k + 1) * FEAT], start=True, stop=True)
                    ins.then_inc(pq_ready, 1)
                node_chunks(pe, nothing, chunk)
                pe.wait_ge(ht_copied, CHUNKS)
                pe.wait_ge(p_scaled, CHUNKS)
                pe.wait_ge(q_scaled, CHUNKS)
                pe.wait_ge(idx_done, N_IDX)
                pe.wait_ge(w_done, N_WEIGHTS)
                pass_tensor(pe)
                missed_passes(pe, pass_tensor)

            @block.scalar
            def _(act):
                for k, v in enumerate((ntm_b, norm_b, rtm_b, l1_b, norm_g)):
                    act.dma_start(cols[:, k:k + 1], v.rearrange("(f a) -> f a", a=1)).then_inc(bc_in, 16)
                act.dma_start(l2b_row[:, :], l2_b.rearrange("(a f) -> a f", a=1)).then_inc(bc_in, 16)
                act.dma_start(lng_b[:, :], ln_g.rearrange("(a f) -> a f", a=1).to_broadcast([P, FEAT]))\
                   .then_inc(bc_in, 16)
                act.dma_start(lnb_b[:, :], ln_b.rearrange("(a f) -> a f", a=1).to_broadcast([P, FEAT]))\
                   .then_inc(bc_in, 16)
                act.wait_ge(consts, N_CONSTS)

                def normalise(c, slot, tiles, rows):
                    act.wait_ge(var_ready, c + 1)
                    nc.scalar.activation(rs[0:rows, slot, 1, 0:tiles], rs[0:rows, slot, 0, 0:tiles], ACT.Sqrt)\
                      .then_inc(sd_ready, 1)
                    act.wait_ge(norm_ready, c + 1)
                    if not (isinstance(c, int) and c < 2):
                        act.wait_ge(ht_ready, c - 1)
                    for t in range(tiles):
                        xt = x_s[0:rows, bass.ds(c * CT + t, 1), :].rearrange("p a h -> p (a h)")
                        ins = nc.scalar.activation(h_s[0:rows, slot, t, :], xt, ACT.Relu,
                                                   bias=rs[0:rows, slot, 5, t:t + 1],
                                                   scale=rs[0:rows, slot, 4, t:t + 1])
                    ins.then_inc(h_ready, 1)

                def chunk(c, slot, tiles, rows):
                    n = (tiles - 1) * P + rows
                    act.wait_ge(y_ready, c + 1)
                    if isinstance(c, int) and c == 0:
                        act.wait_ge(w_done, 15)
                    if not (isinstance(c, int) and c < 2):
                        act.wait_ge(pq_ready, c - 1)
                    nc.scalar.activation(yc_s[:, slot, 0:n], y_ps[:, slot, 0:n], ACT.Identity,
                                         bias=ntm_bc[:, 0:1]).then_inc(yc_ready, 1)
                    nc.scalar.activation(ysq_s[:, slot, 0:n], y_ps[:, slot, 0:n], ACT.Square,
                                         bias=ntm_bc[:, 0:1]).then_inc(yc_ready, 1)
                    act.wait_ge(ssv_ready, c + 1)
                    nc.scalar.activation(rs2[0:rows, slot, 1, 0:tiles], rs2[0:rows, slot, 0, 0:tiles], ACT.Sqrt)\
                      .then_inc(sd2_ready, 1)
                    act.wait_ge(r2_ready, c + 1)
                    if not (isinstance(c, int) and c < 2):
                        act.wait_ge(p_out[slot], slot_loaded(c - 2, slot))
                    for t in range(tiles):
                        ins = nc.scalar.activation(pq_s[0:rows, slot, t, 0:FEAT], pq_ps[0:rows, 0, t, :],
                                                   ACT.Copy, scale=rs2[0:rows, slot, 4, t:t + 1])
                    ins.then_inc(p_scaled, 1)
                node_chunks(act, normalise, chunk)
                pass_scalar(act)
                missed_passes(act, pass_scalar)

            @block.vector
            def _(dve):
                def copied(ins):
                    ins.then_inc(w_done, 1)
                copied(nc.vector.memset(win_q[64:P, :, :], 0.0))
                dve.wait_ge(bc_in, 16 * 8)
                dve.wait_ge(consts, N_CONSTS)
                n = 0

                def product_ready():
                    nonlocal n
                    n += 1
                    dve.wait_ge(w_mm, n)
                for dest in (ntm_t[:, 0, :], ntm_t[:, 1, :], l1_t[:, 0, :], l1_t[:, 1, :], l1_t[:, 2, :]):
                    product_ready()
                    copied(nc.vector.tensor_copy(dest, set_ps[:, 0:P]))
                dve.wait_ge(w_done, 6)
                for k in range(2):
                    copied(nc.vector.tensor_scalar(ab_t[:, k * FEAT:(k + 1) * FEAT], l1_t[:, k, :],
                                                   cols[:, 4:5], None, ALU.mult))
                for k in range(3):
                    copied(nc.vector.tensor_scalar(vec_rep[:, k, :], ones[:, :], cols[:, 1 + k:2 + k], None,
                                                   ALU.mult))
                product_ready()
                copied(nc.vector.tensor_copy(q_bias[:, :], set_ps[:, 0:P]))
                product_ready()
                dve.wait_ge(w_done, 12)
                for s in range(2):
                    copied(nc.vector.tensor_copy(win_q[RBF_ROW:P, s, :], set_ps[RBF_ROW:P, 0:P]))
                product_ready()
                copied(nc.vector.tensor_copy(ntm_bc[:, :], set_ps[:, 0:1]))
                for dest in (mtn_t[:, 0:P], mtn_t[:, P:HID], l2_t[:, :]):
                    product_ready()
                    copied(nc.vector.tensor_copy(dest, set_ps[:, 0:P]))

                dve.wait_ge(idx_in, 16)
                nc.vector.tensor_copy(dst_f[:, :], dst_i[:, :]).then_inc(idx_done, 1)
                nc.vector.tensor_copy(base[:, :], dst_i[0:1, ::GT]).then_inc(idx_done, 1)
                dve.wait_ge(idx_done, 1)
                product_ready()
                nc.vector.tensor_tensor(rel[:, :].rearrange("p (g t) -> p g t", t=GT),
                                        dst_f[:, :].rearrange("p (g t) -> p g t", t=GT),
                                        set_ps[:, 0:GROUPS].unsqueeze(2).to_broadcast([P, GROUPS, GT]),
                                        ALU.subtract).then_inc(idx_done, 1)
                dve.wait_ge(idx_done, 3)
                nc.vector.tensor_scalar(miss[:, :], rel[:, :], 0.0, None, ALU.is_lt).then_inc(idx_done, 1)
                dve.wait_ge(idx_done, 4)
                nc.vector.scalar_tensor_tensor(miss[:, :], rel[:, :], float(WIN), miss[:, :], ALU.is_ge, ALU.add,
                                               accum_out=miss_n[:, 0:1]).then_inc(idx_done, 1)
                product_ready()
                nc.vector.tensor_copy(miss_i[:, :], set_ps[0:1, 0:1]).then_inc(idx_done, 1)

                def refined_rsqrt(step, done_before, w, rows, tiles, last_sem):
                    v, sd, r, t, res = (w[0:rows, k, 0:tiles] for k in range(5))
                    nc.vector.reciprocal(r, sd).then_inc(step, 1)
                    dve.wait_ge(step, done_before + 1)
                    nc.vector.tensor_tensor(t, r, r, ALU.mult).then_inc(step, 1)
                    dve.wait_ge(step, done_before + 2)
                    nc.vector.scalar_tensor_tensor(t, t, -0.5, v, ALU.mult, ALU.mult).then_inc(step, 1)
                    dve.wait_ge(step, done_before + 3)
                    nc.vector.scalar_tensor_tensor(res, t, 1.5, r, ALU.add, ALU.mult).then_inc(last_sem, 1)

                def statistics(c, slot, tiles, rows):
                    dve.wait_ge(x_in[slot], slot_loaded(c, slot))
                    for t in range(tiles):
                        xt = x_s[0:rows, bass.ds(c * CT + t, 1), :].rearrange("p a h -> p (a h)")
                        ins = nc.vector.bn_stats(bn6[0:rows, slot, t, :], xt)
                    ins.then_inc(bn_step, 1)
                    dve.wait_ge(bn_step, 2 * c + 1)
                    dve.sem_inc(aggr_turn, 1)
                    for t in range(tiles):
                        ins = nc.vector.bn_aggr(mv[0:rows, slot, t, :], bn6[0:rows, slot, t, :])
                    ins.then_inc(bn_step, 1)
                    dve.wait_ge(bn_step, 2 * c + 2)
                    if not (isinstance(c, int) and c < 2):
                        dve.wait_ge(h_ready, c - 1)
                    nc.vector.tensor_scalar(rs[0:rows, slot, 0, 0:tiles], mv[0:rows, slot, 0:tiles, 1], EPS, None,
                                            ALU.add).then_inc(var_ready, 1)
                    dve.wait_ge(var_ready, c + 1)
                    dve.wait_ge(sd_ready, c + 1)
                    refined_rsqrt(r_step, 4 * c, rs[:, slot, :, :], rows, tiles, r_step)
                    dve.wait_ge(r_step, 4 * c + 4)
                    nc.vector.scalar_tensor_tensor(rs[0:rows, slot, 5, 0:tiles], mv[0:rows, slot, 0:tiles, 0], -1.0,
                                                   rs[0:rows, slot, 4, 0:tiles], ALU.mult, ALU.mult)\
                      .then_inc(norm_ready, 1)

                def chunk(c, slot, tiles, rows):
                    n = (tiles - 1) * P + rows
                    dve.wait_ge(ht_ready, c + 1)
                    if not (isinstance(c, int) and c < 2):
                        dve.wait_ge(y_ready, c - 1)
                    nc.vector.tensor_copy(ht_s[:, slot, :, 0:n], ht_ps[:, :, 0:n]).then_inc(ht_copied, 1)
                    dve.wait_ge(pq_ready, c + 1)
                    if not (isinstance(c, int) and c < 2):
                        dve.wait_ge(p_scaled, c - 1)
                        dve.wait_ge(q_scaled, c - 1)
                    nc.vector.tensor_scalar(rs2[0:rows, slot, 0, 0:tiles], ss_ps[0:rows, 0:tiles], 1.0 / FEAT, EPS,
                                            ALU.mult, ALU.add).then_inc(ssv_ready, 1)
                    dve.wait_ge(ssv_ready, c + 1)
                    dve.wait_ge(sd2_ready, c + 1)
                    refined_rsqrt(r2_step, 3 * c, rs2[:, slot, :, :], rows, tiles, r2_ready)
                    dve.wait_ge(r2_ready, c + 1)
                    if not (isinstance(c, int) and c < 2):
                        dve.wait_ge(q_out[slot], slot_loaded(c - 2, slot))
                    for t in range(tiles):
                        ins = nc.vector.scalar_tensor_tensor(
                            pq_s[0:rows, slot, t, FEAT:2 * FEAT], pq_ps[0:rows, 1, t, :],
                            rs2[0:rows, slot, 4, t:t + 1], q_bias[0:rows, :], ALU.mult, ALU.add)
                    ins.then_inc(q_scaled, 1)
                node_chunks(dve, statistics, chunk)
                dve.wait_ge(acc_zero, 1)
                pass_vector(dve)
                missed_passes_vector(dve)

        with nc.Block() as block:
            def over_chunks(eng, chunk):
                for c in range(2):
                    chunk(c, c, CT, P)
                with eng.Fori(0, (FULL_CHUNKS - 2) // 2) as i:
                    for j in range(2):
                        chunk(2 * i + (2 + j), j, CT, P)
                chunk(FULL_CHUNKS, FULL_CHUNKS % 2, 1, LAST_ROWS)

            def result_ps(slot):
                return pre_ps[:, slot, :].rearrange("p (t h) -> p t h", t=CT)

            @block.tensor
            def _(pe):
                def chunk(c, slot, tiles, rows):
                    n = (tiles - 1) * P + rows
                    nodes = bass.ds(c * CHUNK, n)
                    if not (isinstance(c, int) and c < 2):
                        pe.wait_ge(msg_copied, c - 1)
                    nc.tensor.matmul(agg_ps[:, slot, 0:n], l2_t[:, :], acc[:, 0, nodes], start=True, stop=False)
                    nc.tensor.matmul(agg_ps[:, slot, 0:n], l2b_row[:, :], acc[0:1, 1, nodes],
                                     start=False, stop=True).then_inc(msg_ready, 1)
                    pe.wait_ge(msg_copied, c + 1)
                    if not (isinstance(c, int) and c < 2):
                        pe.wait_ge(fin_ready, c - 1)
                    for t in range(tiles):
                        ins = nc.tensor.matmul(result_ps(slot)[0:rows, t, :], msg_s[:, slot, t * P:t * P + rows],
                                               mtn_t[:, :], start=True, stop=True)
                    ins.then_inc(out_ready, 1)
                over_chunks(pe, chunk)

            @block.scalar
            def _(act):
                def chunk(c, slot, tiles, rows):
                    n = (tiles - 1) * P + rows
                    act.wait_ge(msg_ready, c + 1)
                    if not (isinstance(c, int) and c < 2):
                        act.wait_ge(out_ready, c - 1)
                    nc.scalar.activation(msg_s[:, slot, 0:n], agg_ps[:, slot, 0:n], ACT.Copy)\
                      .then_inc(msg_copied, 1)
                over_chunks(act, chunk)

            @block.vector
            def _(dve):
                def chunk(c, slot, tiles, rows):
                    dve.wait_ge(out_ready, c + 1)
                    if not (isinstance(c, int) and c < 2):
                        dve.wait_ge(o_out[slot], slot_loaded(c - 2, slot))
                    nc.vector.tensor_tensor(fin[0:rows, slot, 0:tiles, :], result_ps(slot)[0:rows, 0:tiles, :],
                                            x_s[0:rows, bass.ds(c * CT, tiles), :], ALU.add)\
                      .then_inc(fin_ready, 1)
                over_chunks(dve, chunk)

            @block.sync
            def _(sp):
                def chunk(c, slot, tiles, rows):
                    sp.wait_ge(fin_ready, c + 1)
                    if tiles == CT:
                        sp.dma_start(out[bass.ds(c * CHUNK, CHUNK), :].rearrange("(t p) h -> p t h", p=P),
                                     fin[:, slot, :, :]).then_inc(o_out[slot], 16)
                    else:
                        sp.dma_start(out[c * CHUNK:NODES, :], fin[0:rows, slot, 0, :])\
                          .then_inc(o_out[slot], 16)
                over_chunks(sp, chunk)
                for slot in range(2):
                    last = CHUNKS - 1 if (CHUNKS - 1) % 2 == slot else CHUNKS - 2
                    sp.wait_ge(o_out[slot], slot_loaded(last, slot))


def kernel(x, src, dst, edge_attr_32, L0_gnn_ntm_w, L0_gnn_ntm_b, L0_gnn_rtm_w, L0_gnn_rtm_b,
           L0_gnn_norm_g, L0_gnn_norm_b, L0_gnn_l1_w, L0_gnn_l1_b, L0_gnn_ln_g, L0_gnn_ln_b,
           L0_gnn_l2_w, L0_gnn_l2_b, L0_gnn_mtn_w):
    import numpy as np
    import concourse.bacc as bacc
    from concourse.bass_utils import run_bass_kernel_spmd

    def tiles_of(index, filler):
        padded = np.full(PAD_EDGES, filler, np.int32)
        padded[:EDGES] = index
        return np.ascontiguousarray(padded.reshape(EDGE_TILES, P).T)

    src_t = tiles_of(np.asarray(src), 0).reshape(P, PAIRS, 2 * GT).transpose(1, 0, 2)
    rbf_t = np.zeros((RBF, PAD_EDGES), np.float32)
    rbf_t[:, :EDGES] = np.asarray(edge_attr_32).T
    arrays = {
        "x": x, "src": src_t, "dst": tiles_of(np.asarray(dst), NODES), "rbf_t": rbf_t,
        "ntm_w": L0_gnn_ntm_w, "ntm_b": L0_gnn_ntm_b, "rtm_w": L0_gnn_rtm_w, "rtm_b": L0_gnn_rtm_b,
        "norm_g": L0_gnn_norm_g, "norm_b": L0_gnn_norm_b, "l1_w": L0_gnn_l1_w, "l1_b": L0_gnn_l1_b,
        "ln_g": L0_gnn_ln_g, "ln_b": L0_gnn_ln_b, "l2_w": L0_gnn_l2_w, "l2_b": L0_gnn_l2_b,
        "mtn_w": L0_gnn_mtn_w,
    }
    arrays = {f"in_{k}": np.ascontiguousarray(v) for k, v in arrays.items()}
    nc = bacc.Bacc("TRN2", target_bir_lowering=False, num_devices=1)
    args = [nc.dram_tensor(k, a.shape, mybir.dt.from_np(a.dtype), kind="ExternalInput").ap()
            for k, a in arrays.items()]
    out = nc.dram_tensor("out", (NODES, HID), F32, kind="ExternalOutput").ap()
    bass_gnn_layer(nc, *args, out)
    result = run_bass_kernel_spmd(nc, [arrays], core_ids=[0])
    return result.results[0]["out"]
```

```python
from contextlib import ExitStack

import concourse.bass as bass
from concourse import mybir

ALU = mybir.AluOpType
ACT = mybir.ActivationFunctionType
F32 = mybir.dt.float32
BF16 = mybir.dt.bfloat16
I32 = mybir.dt.int32
U32 = mybir.dt.uint32

P = 128
EPS = 1e-5
NODES, HID, FEAT, RBF = 6250, 256, 128, 32
EDGES = 106250

CT = 4
CHUNK = CT * P
FULL_CHUNKS = NODES // CHUNK
LAST_ROWS = NODES - FULL_CHUNKS * CHUNK
CHUNKS = FULL_CHUNKS + 1
NODE_TILES = FULL_CHUNKS * CT + 1
assert 0 < LAST_ROWS <= P

LAG_STATS, LAG_RELU, LAG_TRANSPOSE, LAG_Y, LAG_PQ, LAG_SCALE = range(6)
STEPS = CHUNKS + LAG_SCALE
HEAD_STEPS = LAG_SCALE + 1
LOOP_STEPS = (FULL_CHUNKS - HEAD_STEPS) // 2 * 2

GT = 8
HALF = GT // 2
GROUP = GT * P
PAIRS = -(-EDGES // (2 * GROUP))
GROUPS = 2 * PAIRS
EDGE_TILES = GROUPS * GT
PAD_EDGES = EDGE_TILES * P
HEAD_PAIRS, TAIL_PAIRS = 2, 2
assert PAIRS % 2 == 0 and (PAIRS - HEAD_PAIRS - TAIL_PAIRS) % 2 == 0

WIN = 80
RBF_ROW = 96
TABLE_ROWS = 6400
WINDOWS = -(-NODES // WIN)
assert NODES + WIN <= TABLE_ROWS and WINDOWS * WIN <= TABLE_ROWS

RSQRT_MAGIC = 0x5F3759DF
NT_STEPS = 12
N_MASKS = 4
N_CONSTS = 4
EARLY_WEIGHTS, N_WEIGHTS = 9, 12
N_IDX = 6
ENGINES = 5
HANDLED = -1.0e6


def bass_gnn_layer(nc, x, src, dst, rbf_t, ntm_w, ntm_b, rtm_w, rtm_b, norm_g, norm_b,
                   l1_w, l1_b, ln_g, ln_b, l2_w, l2_b, mtn_w, out):
    with ExitStack() as ctx:
        def sb(name, shape, dt=F32):
            return ctx.enter_context(nc.sbuf_tensor(name, shape, dt))

        def psum(name, shape):
            return ctx.enter_context(nc.psum_tensor(name, shape, F32))

        def sem(name):
            return ctx.enter_context(nc.semaphore(name))

        p_table = nc.dram_tensor("p_table", [NODES, FEAT], F32, kind="Internal").ap()
        q_table = nc.dram_tensor("q_table", [TABLE_ROWS, FEAT], F32, kind="Internal").ap()

        ident = sb("ident", [P, P])
        ident_bf = sb("ident_bf", [P, P], BF16)
        center = sb("center", [P, P])
        ones = sb("ones", [P, P])
        ones_bf = sb("ones_bf", [P, P], BF16)
        iota = sb("iota", [P, WIN])
        ntm_s = sb("ntm_s", [FEAT, HID])
        l1_s = sb("l1_s", [FEAT, 3 * FEAT])
        rtm_s = sb("rtm_s", [FEAT, P])
        l2_s = sb("l2_s", [FEAT, FEAT])
        mtn_s = sb("mtn_s", [P, 2, FEAT])
        cols = sb("cols", [P, 8])
        lng_b = sb("lng_b", [P, FEAT])
        lnb_b = sb("lnb_b", [P, FEAT])
        ntm_t = sb("ntm_t", [P, 2, FEAT])
        l1_t = sb("l1_t", [P, 3, FEAT])
        ab_t = sb("ab_t", [P, 2 * FEAT])
        vec_rep = sb("vec_rep", [P, 3, P])
        q_bias = sb("q_bias", [P, FEAT])
        ntm_bc = sb("ntm_bc", [P, 1])
        ml_t = sb("ml_t", [P, HID + FEAT])
        mtn_t, l2_t = ml_t[:, 0:HID], ml_t[:, HID:HID + FEAT]

        x_s = sb("x_s", [P, NODE_TILES, HID])
        bn6 = sb("bn6", [P, 2, CT, 6])
        mv = sb("mv", [P, 2, CT, 2])
        rs = sb("rs", [P, 2, 6, 2 * CT])
        pq_s = sb("pq_s", [P, 2, CT, 2 * FEAT])

        src_s = sb("src_s", [P, 2, 2 * GT], I32)
        dst_i = sb("dst_i", [P, EDGE_TILES], I32)
        dst_f = sb("dst_f", [P, EDGE_TILES])
        rel = sb("rel", [P, EDGE_TILES])
        miss = sb("miss", [P, EDGE_TILES])
        miss_n = sb("miss_n", [P, 2])
        base = sb("base", [1, GROUPS], I32)
        miss_i = sb("miss_i", [1, 1], I32)
        acc = sb("acc", [P, TABLE_ROWS])
        win_sum = sb("win_sum", [P, 2, WIN])
        gath = sb("gath", [P, 2, 2, GT, FEAT])
        onehot = sb("onehot", [P, 4, GT, WIN])
        edge_t = sb("edge_t", [P, 2, GROUP])
        win_q = sb("win_q", [P, 2, FEAT])
        z = sb("z", [P, 2, 2, GT, FEAT])
        ssum = sb("ssum", [P, 2, 2 * GT])
        nt = sb("nt", [P, 3, 2 * GT])
        gel = sb("gel", [P, 2, GT, FEAT])
        h_s = z[:, 0, :, :, :].rearrange("p s t f -> p s (t f)").rearrange("p s (t h) -> p s t h", t=CT)
        ht_s = z[:, 1, :, :, :].rearrange("p s t f -> p s (t f)").rearrange("p s (k n) -> p s k n", k=2)
        yc_s = gath[:, 1, 0, :, :].rearrange("p t f -> p (t f)").rearrange("p (s n) -> p s n", s=2)
        ysq_s = gath[:, 1, 1, :, :].rearrange("p t f -> p (t f)").rearrange("p (s n) -> p s n", s=2)
        msg_s = gath[:, 0, 0, :, :].rearrange("p t f -> p (t f)").rearrange("p (s n) -> p s n", s=2)

        pre_ps = psum("pre_ps", [P, 2, GROUP])
        oht_ps = psum("oht_ps", [P, GROUP])
        agg_ps = psum("agg_ps", [P, 2, 512])
        pq_ps = pre_ps[:, :, :].rearrange("p s (k t f) -> p s k t f", k=2, t=CT)
        ht_ps = oht_ps[:, :].rearrange("p (k n) -> p k n", k=2)
        y_ps = agg_ps[:, 0, :]
        ss_ps = agg_ps[:, 1, :]
        ntm_ps, ntm_b_ps = agg_ps[:, 1, 0:HID], agg_ps[:, 0, 0:1]
        l1_ps = pre_ps[:, 0, 0:3 * FEAT]
        ml_ps = pre_ps[:, 1, 0:HID + FEAT]
        bias_ps, wr_ps = pre_ps[:, 1, 512:512 + FEAT], pre_ps[:, 1, 512 + FEAT:512 + 2 * FEAT]
        base_ps, miss_ps = oht_ps[:, 0:GROUPS], oht_ps[0:1, 512:514]

        w_in = sem("w_in")
        late_w_in = sem("late_w_in")
        cols_in = sem("cols_in")
        bc_in = sem("bc_in")
        idx_in = sem("idx_in")
        masks = sem("masks")
        eye_ready = sem("eye_ready")
        rs_set = sem("rs_set")
        consts = sem("consts")
        w_mm = sem("w_mm")
        w_done = sem("w_done")
        idx_mm = sem("idx_mm")
        idx_done = sem("idx_done")
        acc_zero = sem("acc_zero")
        zero_out = sem("zero_out")
        x_in = [sem("x_in0"), sem("x_in1")]
        bn_step = sem("bn_step")
        aggr_turn = sem("aggr_turn")
        var_ready = sem("var_ready")
        var2_ready = sem("var2_ready")
        sd_ready = sem("sd_ready")
        r_step = sem("r_step")
        norm_ready = sem("norm_ready")
        h_ready = sem("h_ready")
        ht_ready = sem("ht_ready")
        ht_copied = [sem("ht_copied0"), sem("ht_copied1")]
        y_ready = sem("y_ready")
        yc_ready = sem("yc_ready")
        pq_ready = sem("pq_ready")
        p_scaled = sem("p_scaled")
        q_scaled = sem("q_scaled")
        p_out = [sem("p_out0"), sem("p_out1")]
        q_out = [sem("q_out0"), sem("q_out1")]
        s_ready = sem("s_ready")
        oht_ready = sem("oht_ready")
        oht_copied = sem("oht_copied")
        src_in = [sem("src_in0"), sem("src_in1")]
        rbf_in = [sem("rbf_in0"), sem("rbf_in1")]
        q_in = [sem("q_in0"), sem("q_in1")]
        pre_ready = sem("pre_ready")
        gathered = [[[sem(f"gathered{s}{h}{a}") for a in range(2)] for h in range(2)] for s in range(2)]
        gather_turn = sem("gather_turn")
        sum_ready = sem("sum_ready")
        ssum_ready = sem("ssum_ready")
        nt_step = sem("nt_step")
        norm_step = sem("norm_step")
        z_ready = sem("z_ready")
        gelu_ready = sem("gelu_ready")
        agg_ready = sem("agg_ready")
        sums_copied = sem("sums_copied")
        msg_ready = sem("msg_ready")
        agg_added = sem("agg_added")
        pass_sems = [s_ready, oht_ready, oht_copied, *src_in, *rbf_in, *q_in, pre_ready,
                     gather_turn, sum_ready, ssum_ready, nt_step, norm_step, z_ready, gelu_ready, agg_ready,
                     sums_copied, msg_ready, agg_added]
        pass_end = sem("pass_end")
        windows_set = sem("windows_set")
        win_step = sem("win_step")
        clear_turn = sem("clear_turn")
        pass_begun = sem("pass_begun")
        reset_asked = sem("reset_asked")
        reset_begun = sem("reset_begun")
        gathers_reset = sem("gathers_reset")
        out_ready = sem("out_ready")
        msg_copied = sem("msg_copied")
        fin_ready = sem("fin_ready")
        o_out = sem("o_out")

        def slot_loaded(n, slot):
            return 16 * ((n - slot) // 2 + 1) if isinstance(n, int) else 8 * (n - slot) + 16

        def over_pairs(eng, pair):
            for p in range(HEAD_PAIRS):
                pair(p, p % 2, p == 0, False, False)
            with eng.Fori(0, (PAIRS - HEAD_PAIRS - TAIL_PAIRS) // 2) as i:
                for j in range(2):
                    pair(2 * i + (HEAD_PAIRS + j), j, False, True, False)
            for p in range(PAIRS - TAIL_PAIRS, PAIRS):
                pair(p, p % 2, False, True, p == PAIRS - 1)

        def pass_sync(sp):
            def loads(g, h, warm):
                start = sp.value_load(base[0:1, bass.ds(g, 1)], min_val=0, max_val=NODES)
                if warm:
                    sp.wait_ge(pre_ready, g - 1)
                sp.dma_start(edge_t[RBF_ROW:P, h, :], rbf_t[:, bass.ds(g * GROUP, GROUP)])\
                  .then_inc(rbf_in[h], 16)
                sp.dma_start(win_q[0:WIN, h, :], q_table[bass.ds(start, WIN), :])\
                  .then_inc(q_in[h], 16)

            def sources(p, par):
                sp.dma_start(src_s[:, par, :], src[bass.ds(p, 1), :, :].rearrange("a p t -> (a p) t"))\
                  .then_inc(src_in[par], 16)

            def pair(p, par, first, warm, last):
                for h in range(2):
                    loads(2 * p + h, h, not first)
                if not last:
                    if not first:
                        for h in range(2):
                            for a in range(2):
                                sp.wait_ge(gathered[1 - par][h][a], HALF * slot_loaded(p - 1, 1 - par))
                    sources(p + 1, 1 - par)

            sources(0, 0)
            over_pairs(sp, pair)

        def pass_gpsimd(pool):
            def pair(p, par, first, warm, last):
                pool.wait_ge(src_in[par], slot_loaded(p, par))
                for h in range(2):
                    g = 2 * p + h
                    if warm:
                        pool.wait_ge(sum_ready, 2 * g - 6)
                    pool.sem_inc(gather_turn, 1)
                    for t in range(GT):
                        pool.indirect_dma_start(
                            out=gath[:, par, h, t, :], out_offset=None, in_=p_table,
                            in_offset=bass.IndirectOffsetOnAxis(
                                ap=src_s[:, par, h * GT + t:h * GT + t + 1].bitcast(U32), axis=0),
                        ).then_inc(gathered[par][h][t // (GT // 2)], 16)
            over_pairs(pool, pair)

        def msg_ps(h):
            return agg_ps[:, h, 2 * WIN:3 * WIN]

        def pass_vector(dve):
            def one_hot(g, slot, reused):
                if reused:
                    dve.wait_ge(agg_ready, g - 3)
                nc.vector.tensor_tensor(
                    onehot[:, slot, :, :],
                    iota[:, :].unsqueeze(1).to_broadcast([P, GT, WIN]),
                    rel[:, bass.ds(g * GT, GT)].unsqueeze(2).to_broadcast([P, GT, WIN]),
                    ALU.is_equal).then_inc(s_ready, 1)

            def window_start(g):
                return dve.value_load(base[0:1, bass.ds(g, 1)], min_val=0, max_val=NODES)

            def add_count_term(g, h, start):
                dve.wait_ge(msg_ready, g + 1)
                if not (isinstance(g, int) and g == 0):
                    dve.wait_ge(agg_added, 2 * g)
                window = acc[:, bass.ds(start, WIN)]
                nc.vector.scalar_tensor_tensor(window, agg_ps[:, h, WIN:2 * WIN], cols[:, 5:6], window,
                                               ALU.mult, ALU.add).then_inc(agg_added, 1)

            def add_messages(g, h, start):
                dve.wait_ge(agg_added, 2 * g + 1)
                window = acc[:, bass.ds(start, WIN)]
                nc.vector.tensor_tensor(window, window, msg_ps(h), ALU.add).then_inc(agg_added, 1)

            def add_sums(g, h):
                start = window_start(g)
                add_count_term(g, h, start)
                add_messages(g, h, start)

            def add_gathered(p, par, h, warm):
                g = 2 * p + h
                dve.wait_ge(pre_ready, g + 1)
                if warm:
                    dve.wait_ge(gelu_ready, 2 * g - 6)
                for a in range(2):
                    t = slice(a * HALF, (a + 1) * HALF)
                    dve.wait_ge(gathered[par][h][a], HALF * slot_loaded(p, par))
                    nc.vector.tensor_tensor(
                        z[:, par, h, t, :],
                        pre_ps[:, h, :].rearrange("p (t f) -> p t f", t=GT)[:, t, :],
                        gath[:, par, h, t, :], ALU.add).then_inc(sum_ready, 1)

            def rstd_step(p, par, h, n):
                done = NT_STEPS * (2 * p + h) + n
                tiles = slice(h * GT, (h + 1) * GT)
                var, y, t = nt[:, 0, tiles], nt[:, 1, tiles], nt[:, 2, tiles]
                if n == 0:
                    dve.wait_ge(ssum_ready, 2 * p + h + 1)
                    ins = nc.vector.tensor_scalar(var, ssum[:, par, tiles], 1.0 / FEAT, EPS, ALU.mult, ALU.add)
                else:
                    dve.wait_ge(nt_step, done)
                    if n == 1:
                        ins = nc.vector.tensor_scalar(t.bitcast(I32), var.bitcast(I32), 1, None,
                                                      ALU.logical_shift_right)
                    elif n == 2:
                        ins = nc.vector.tensor_scalar(y.bitcast(I32), t.bitcast(I32), -1.0,
                                                      float(RSQRT_MAGIC), ALU.mult, ALU.add)
                    elif n % 3 == 0:
                        ins = nc.vector.tensor_tensor(t, y, y, ALU.mult)
                    elif n % 3 == 1:
                        ins = nc.vector.scalar_tensor_tensor(t, t, -0.5, var, ALU.mult, ALU.mult)
                    else:
                        ins = nc.vector.scalar_tensor_tensor(y, t, 1.5, y, ALU.add, ALU.mult)
                ins.then_inc(nt_step, 1)

            def normalise(p, par, h, beside_rstd):
                n = 0
                dve.wait_ge(nt_step, NT_STEPS * (2 * p + h + 1))
                for a in range(2):
                    for t in range(a * HALF, (a + 1) * HALF):
                        if beside_rstd:
                            rstd_step(p, par, h + 1, n)
                            n += 1
                        ins = nc.vector.scalar_tensor_tensor(
                            z[:, par, h, t, :], z[:, par, h, t, :], nt[:, 1, h * GT + t:h * GT + t + 1],
                            lng_b[:, :], ALU.mult, ALU.mult)
                    ins.then_inc(norm_step, 1)
                    if beside_rstd:
                        rstd_step(p, par, h + 1, n)
                        n += 1
                    dve.wait_ge(norm_step, 4 * p + (2 * h + a + 1))
                    t = slice(a * HALF, (a + 1) * HALF)
                    nc.vector.tensor_tensor(
                        z[:, par, h, t, :], z[:, par, h, t, :],
                        lnb_b[:, :].unsqueeze(1).to_broadcast([P, HALF, FEAT]),
                        ALU.add).then_inc(z_ready, 1)
                if beside_rstd:
                    for n in range(n, NT_STEPS):
                        rstd_step(p, par, h + 1, n)

            def pair(p, par, first, warm, last):
                if last:
                    for h in range(2):
                        add_gathered(p, par, h, warm)
                        if h == 1:
                            for before in range(2):
                                add_sums(2 * p - 2 + before, before)
                        for n in range(NT_STEPS):
                            rstd_step(p, par, h, n)
                        normalise(p, par, h, False)
                    return
                starts = []
                for h in range(2):
                    add_gathered(p, par, h, warm)
                    one_hot(2 * p + 2 + h, (2 * par + h + 2) % 4, not first)
                    if not first:
                        starts.append(window_start(2 * p - 2 + h))
                for n in range(NT_STEPS):
                    rstd_step(p, par, 0, n)
                    if not first and n >= NT_STEPS - 4:
                        h, part = divmod(n - (NT_STEPS - 4), 2)
                        (add_messages if part else add_count_term)(2 * p - 2 + h, h, starts[h])
                normalise(p, par, 0, True)
                normalise(p, par, 1, False)

            one_hot(0, 0, False)
            one_hot(1, 1, False)
            over_pairs(dve, pair)
            for h in range(2):
                add_sums(GROUPS - 2 + h, h)

        def pass_scalar(act):
            def copy_one_hot(g, h, reused):
                act.wait_ge(oht_ready, g + 1)
                if reused:
                    act.wait_ge(pre_ready, g - 1)
                nc.scalar.activation(edge_t[0:WIN, h, :], oht_ps[0:WIN, :], ACT.Copy)\
                  .then_inc(oht_copied, 1)

            def copy_sums(g, h, reused):
                act.wait_ge(agg_ready, g + 1)
                if reused:
                    act.wait_ge(msg_ready, g - 1)
                nc.scalar.activation(win_sum[:, h, :], agg_ps[:, h, 0:WIN], ACT.Copy)\
                  .then_inc(sums_copied, 1)

            def squares(p, par, h, first):
                g = 2 * p + h
                if not first:
                    act.wait_ge(agg_ready, g - 1)
                for t in range(GT):
                    if t % HALF == 0:
                        act.wait_ge(sum_ready, 2 * g + 1 + t // HALF)
                    ins = nc.scalar.activation(gel[:, h, t, :], z[:, par, h, t, :], ACT.Square,
                                               accum_out=ssum[:, par, h * GT + t:h * GT + t + 1])
                ins.then_inc(ssum_ready, 1)

            def gelu(p, par, h):
                g = 2 * p + h
                act.wait_ge(ssum_ready, g + 1)
                for a in range(2):
                    act.wait_ge(z_ready, 2 * g + 1 + a)
                    t = slice(a * HALF, (a + 1) * HALF)
                    nc.scalar.activation(gel[:, h, t, :], z[:, par, h, t, :], ACT.Gelu)\
                      .then_inc(gelu_ready, 1)

            def pair(p, par, first, warm, last):
                for h in range(2):
                    squares(p, par, h, first)
                    if h == 0 and not first:
                        for before in range(2):
                            copy_sums(2 * p - 2 + before, before, warm)
                    if not last:
                        copy_one_hot(2 * p + 2 + h, h, True)
                    if last:
                        gelu(p, par, h)
                if not last:
                    for h in range(2):
                        gelu(p, par, h)

            copy_one_hot(0, 0, False)
            copy_one_hot(1, 1, False)
            over_pairs(act, pair)
            for h in range(2):
                copy_sums(GROUPS - 2 + h, h, True)

        def bf16_view(slot, t):
            return onehot[:, slot, t, :].bitcast(BF16)[:, 1::2]

        def pass_tensor(pe):
            def transposes(g, slot):
                pe.wait_ge(s_ready, g + 1)
                if not (isinstance(g, int) and g == 0):
                    pe.wait_ge(oht_copied, g)
                for t in range(GT):
                    ins = nc.tensor.matmul(oht_ps[0:WIN, t * P:(t + 1) * P], bf16_view(slot, t),
                                           ident_bf[:, :], start=True, stop=True)
                ins.then_inc(oht_ready, 1)

            def product(g, h, reused):
                pe.wait_ge(oht_copied, g + 1)
                pe.wait_ge(rbf_in[h], slot_loaded(g, h))
                pe.wait_ge(q_in[h], slot_loaded(g, h))
                if reused:
                    pe.wait_ge(sum_ready, 2 * g - 2)
                for t in range(GT):
                    ins = nc.tensor.matmul(pre_ps[:, h, t * FEAT:(t + 1) * FEAT],
                                           edge_t[:, h, t * P:(t + 1) * P], win_q[:, h, :],
                                           start=True, stop=True)
                ins.then_inc(pre_ready, 1)

            def sums(g, h, slot, reused):
                if reused:
                    pe.wait_ge(agg_added, 2 * g - 2)
                for t in range(GT):
                    if t % HALF == 0:
                        pe.wait_ge(gelu_ready, 2 * g + 1 + t // HALF)
                    nc.tensor.matmul(agg_ps[:, h, 0:WIN], gel[:, h, t, :], onehot[:, slot, t, :],
                                     start=(t == 0), stop=(t == GT - 1), skip_group_check=True)
                    ins = nc.tensor.matmul(agg_ps[:, h, WIN:2 * WIN], ones_bf[:, :], bf16_view(slot, t),
                                           start=False, stop=(t == GT - 1), skip_group_check=True)
                ins.then_inc(agg_ready, 1)

            def messages(g, h):
                pe.wait_ge(sums_copied, g + 1)
                nc.tensor.matmul(msg_ps(h), l2_t, win_sum[:, h, :], start=True, stop=True)\
                  .then_inc(msg_ready, 1)

            def pair(p, par, first, warm, last):
                for h in range(2):
                    if not last:
                        transposes(2 * p + 2 + h, (2 * par + h + 2) % 4)
                    if h == 0 and not first:
                        for before in range(2):
                            messages(2 * p - 2 + before, before)
                    if not last:
                        product(2 * p + 2 + h, h, True)
                for h in range(2):
                    sums(2 * p + h, h, 2 * par + h, not first)

            for h in range(2):
                transposes(h, h)
                product(h, h, False)
            over_pairs(pe, pair)
            for h in range(2):
                messages(GROUPS - 2 + h, h)

        def reset_gathers(pool, r):
            pool.wait_ge(reset_asked, r + 1)
            pool.sem_inc(reset_begun, 1)
            for par in range(2):
                for h in range(2):
                    for a in range(2):
                        pool.wait_ge(gathered[par][h][a], HALF * 16 * (PAIRS // 2))
                        pool.dma_reset(range(gathered[par][h][a].num, gathered[par][h][a].num + 1))
                        pool.sem_clear(gathered[par][h][a])
            pool.sem_inc(gathers_reset, 1)

        def missed_passes(eng, edge_pass, begin=None):
            eng.wait_ge(idx_done, N_IDX)
            missed = eng.value_load(miss_i[0:1, 0:1], min_val=0, max_val=PAD_EDGES)
            with eng.If(missed > 0):
                eng.drain().then_inc(pass_end, 1)
                with eng.Fori(0, WINDOWS) as r:
                    if begin:
                        begin(eng, r)
                    eng.wait_ge(windows_set, r + 1)
                    eng.sem_inc(pass_begun, 1)
                    edge_pass(eng)
                    eng.drain().then_inc(pass_end, 1)

        def missed_passes_vector(dve):
            dve.wait_ge(idx_done, N_IDX)
            missed = dve.value_load(miss_i[0:1, 0:1], min_val=0, max_val=PAD_EDGES)
            with dve.If(missed > 0):
                dve.drain().then_inc(pass_end, 1)
                dve.wait_ge(pass_end, ENGINES)
                nc.vector.tensor_scalar(miss[:, :], miss[:, :], -HANDLED, HANDLED + WIN, ALU.mult, ALU.add)\
                  .then_inc(win_step, 1)
                nc.vector.memset(base[:, :], -WIN).then_inc(win_step, 1)
                dve.wait_ge(win_step, 2)
                nc.vector.tensor_tensor(rel[:, :], dst_f[:, :], miss[:, :], ALU.add).then_inc(win_step, 1)
                with dve.Fori(0, WINDOWS) as r:
                    dve.wait_ge(pass_end, ENGINES * r + ENGINES)
                    dve.sem_inc(clear_turn, 1)
                    for s in pass_sems:
                        dve.sem_clear(s)
                    dve.sem_inc(reset_asked, 1)
                    dve.wait_ge(gathers_reset, r + 1)
                    dve.sem_inc(clear_turn, 1)
                    dve.wait_ge(win_step, 2 * r + 3)
                    nc.vector.tensor_scalar(rel[:, :], rel[:, :], -float(WIN), None, ALU.add)\
                      .then_inc(win_step, 1)
                    nc.vector.tensor_scalar(base[:, :], base[:, :], float(WIN), None, ALU.add)\
                      .then_inc(win_step, 1)
                    dve.wait_ge(win_step, 2 * r + 5)
                    dve.sem_inc(windows_set, 1)
                    pass_vector(dve)
                    dve.drain().then_inc(pass_end, 1)

        def over_chunks(eng, chunk):
            for c in range(2):
                chunk(c, c, CT, P)
            with eng.Fori(0, (FULL_CHUNKS - 2) // 2) as i:
                for j in range(2):
                    chunk(2 * i + (2 + j), j, CT, P)
            chunk(FULL_CHUNKS, FULL_CHUNKS % 2, 1, LAST_ROWS)

        def result_ps(slot):
            return pre_ps[:, slot, :].rearrange("p (t h) -> p t h", t=CT)

        def result_tensor(pe):
            def chunk(c, slot, tiles, rows):
                pe.wait_ge(msg_copied, c + 1)
                if not (isinstance(c, int) and c < 2):
                    pe.wait_ge(fin_ready, c - 1)
                for t in range(tiles):
                    ins = nc.tensor.matmul(result_ps(slot)[0:rows, t, :], msg_s[:, slot, t * P:t * P + rows],
                                           mtn_t, start=True, stop=True)
                ins.then_inc(out_ready, 1)
            pe.wait_ge(sum_ready, 2 * GROUPS)
            over_chunks(pe, chunk)

        def result_scalar(act):
            def chunk(c, slot, tiles, rows):
                n = (tiles - 1) * P + rows
                if not (isinstance(c, int) and c < 2):
                    act.wait_ge(out_ready, c - 1)
                nc.scalar.activation(msg_s[:, slot, 0:n], acc[:, bass.ds(c * CHUNK, n)], ACT.Copy)\
                  .then_inc(msg_copied, 1)
            act.wait_ge(agg_added, 2 * GROUPS)
            over_chunks(act, chunk)

        def result_vector(dve):
            def chunk(c, slot, tiles, rows):
                dve.wait_ge(out_ready, c + 1)
                x_c = x_s[0:rows, bass.ds(c * CT, tiles), :]
                nc.vector.tensor_tensor(x_c, result_ps(slot)[0:rows, 0:tiles, :], x_c, ALU.add)\
                  .then_inc(fin_ready, 1)
            over_chunks(dve, chunk)

        def result_sync(sp):
            def chunk(c, slot, tiles, rows):
                sp.wait_ge(fin_ready, c + 1)
                if tiles == CT:
                    sp.dma_start(out[bass.ds(c * CHUNK, CHUNK), :].rearrange("(t p) h -> p t h", p=P),
                                 x_s[:, bass.ds(c * CT, CT), :]).then_inc(o_out, 16)
                else:
                    sp.dma_start(out[c * CHUNK:NODES, :], x_s[0:rows, c * CT, :]).then_inc(o_out, 16)
            over_chunks(sp, chunk)
            sp.wait_ge(o_out, 16 * CHUNKS)

        def last_of(slot):
            return CHUNKS - 1 if (CHUNKS - 1) % 2 == slot else CHUNKS - 2

        def stored(c, slot):
            return slot_loaded(c, slot) + 16

        def over_steps(eng, step):
            for k in range(HEAD_STEPS):
                step(k, k % 2)
            with eng.Fori(0, LOOP_STEPS // 2) as i:
                for j in range(2):
                    step(2 * i + (HEAD_STEPS + j), (HEAD_STEPS + j) % 2)
            for k in range(HEAD_STEPS + LOOP_STEPS, STEPS):
                step(k, k % 2)

        def is_step(k, n):
            return isinstance(k, int) and k == n

        def chunk_of(k, lag):
            if not isinstance(k, int):
                return k - lag, CT, P
            if not 0 <= k - lag < CHUNKS:
                return None
            return (k - lag, CT, P) if k - lag < FULL_CHUNKS else (k - lag, 1, LAST_ROWS)

        def reused(c):
            return not isinstance(c, int) or c >= 2

        def nodes_tensor(pe):
            def window_starts():
                for half in range(2):
                    pe.wait_ge(ht_copied[half], CHUNKS)
                pe.wait_ge(idx_done, 1)
                nc.tensor.matmul(base_ps, ones[0:1, :], dst_f[0:1, ::GT], start=True, stop=True)\
                  .then_inc(idx_mm, 1)

            def step(k, slot):
                if is_step(k, LAG_Y):
                    pe.wait_ge(w_done, EARLY_WEIGHTS)
                if chunk_of(k, LAG_Y):
                    c, tiles, rows = chunk_of(k, LAG_Y)
                    n = (tiles - 1) * P + rows
                    for half in range(2):
                        pe.wait_ge(ht_copied[half], c + 1)
                    if not (isinstance(c, int) and c < 1):
                        pe.wait_ge(yc_ready, 2 * c)
                    for half in range(2):
                        ins = nc.tensor.matmul(y_ps[:, 0:n], ntm_t[:, half, :], ht_s[:, 1 - slot, half, 0:n],
                                               start=(half == 0), stop=(half == 1))
                    ins.then_inc(y_ready, 1)
                if chunk_of(k, LAG_TRANSPOSE):
                    c, tiles, rows = chunk_of(k, LAG_TRANSPOSE)
                    pe.wait_ge(h_ready, c + 1)
                    if not (isinstance(c, int) and c < 1):
                        for half in range(2):
                            pe.wait_ge(ht_copied[half], c)
                    for t in range(tiles):
                        for half in range(2):
                            ins = nc.tensor.transpose(ht_ps[:, half, t * P:t * P + rows],
                                                      h_s[0:rows, slot, t, half * P:(half + 1) * P],
                                                      ident[0:rows, 0:rows])
                    ins.then_inc(ht_ready, 1)
                if is_step(k, LAG_PQ):
                    pe.wait_ge(w_done, N_WEIGHTS)
                if chunk_of(k, LAG_PQ):
                    c, tiles, rows = chunk_of(k, LAG_PQ)
                    pe.wait_ge(yc_ready, 2 * c + 2)
                    pe.wait_ge(p_scaled, c + 1)
                    pe.wait_ge(q_scaled, c + 1)
                    for t in range(tiles):
                        for part in range(2):
                            nc.tensor.matmul(pq_ps[0:rows, slot, part, t, :], yc_s[:, slot, t * P:t * P + rows],
                                             ab_t[:, part * FEAT:(part + 1) * FEAT], start=True, stop=True)
                    if not (isinstance(c, int) and c < 1):
                        pe.wait_ge(var2_ready, c)
                    for t in range(tiles):
                        ins = nc.tensor.matmul(ss_ps[0:rows, t:t + 1], ysq_s[:, slot, t * P:t * P + rows],
                                               ones[:, 0:1], start=True, stop=True)
                    ins.then_inc(pq_ready, 1)
                if is_step(k, LAG_TRANSPOSE + CHUNKS):
                    window_starts()

            over_steps(pe, step)
            pe.wait_ge(idx_done, 5)
            nc.tensor.matmul(miss_ps, miss_n[:, 0:1], ones[:, 0:2], start=True, stop=True).then_inc(idx_mm, 1)

        def nodes_scalar(act):
            def relu(k, slot, part):
                if chunk_of(k, LAG_RELU):
                    c, tiles, rows = chunk_of(k, LAG_RELU)
                    act.wait_ge(norm_ready, c + 1)
                    if reused(c):
                        act.wait_ge(ht_ready, c - 1)
                    for t in part:
                        if t < tiles:
                            xt = x_s[0:rows, bass.ds(c * CT + t, 1), :].rearrange("p a h -> p (a h)")
                            ins = nc.scalar.activation(h_s[0:rows, 1 - slot, t, :], xt, ACT.Relu,
                                                       bias=rs[0:rows, 1 - slot, 5, t:t + 1],
                                                       scale=rs[0:rows, 1 - slot, 4, t:t + 1])
                            if t == tiles - 1:
                                ins.then_inc(h_ready, 1)

            def step(k, slot):
                if chunk_of(k, LAG_SCALE):
                    c, tiles, rows = chunk_of(k, LAG_SCALE)
                    act.wait_ge(pq_ready, c + 1)
                    act.wait_ge(r_step, 4 * k)
                    act.wait_ge(p_out[1 - slot], slot_loaded(c, 1 - slot))
                    for t in range(tiles):
                        ins = nc.scalar.activation(pq_s[0:rows, 1 - slot, t, 0:FEAT],
                                                   pq_ps[0:rows, 1 - slot, 0, t, :], ACT.Copy,
                                                   scale=rs[0:rows, 1 - slot, 4, CT + t:CT + t + 1])
                    ins.then_inc(p_scaled, 1)
                if is_step(k, LAG_Y):
                    act.wait_ge(w_done, EARLY_WEIGHTS)
                if chunk_of(k, LAG_Y):
                    c, tiles, rows = chunk_of(k, LAG_Y)
                    n = (tiles - 1) * P + rows
                    act.wait_ge(y_ready, c + 1)
                    if reused(c):
                        act.wait_ge(pq_ready, c - 1)
                    nc.scalar.activation(yc_s[:, 1 - slot, 0:n], y_ps[:, 0:n], ACT.Identity,
                                         bias=ntm_bc[:, 0:1]).then_inc(yc_ready, 1)
                    nc.scalar.activation(ysq_s[:, 1 - slot, 0:n], y_ps[:, 0:n], ACT.Square,
                                         bias=ntm_bc[:, 0:1]).then_inc(yc_ready, 1)
                if chunk_of(k, LAG_TRANSPOSE):
                    c, tiles, rows = chunk_of(k, LAG_TRANSPOSE)
                    n = (tiles - 1) * P + rows
                    act.wait_ge(ht_ready, c + 1)
                    if reused(c):
                        act.wait_ge(y_ready, c - 1)
                    nc.scalar.activation(ht_s[:, slot, 1, 0:n], ht_ps[:, 1, 0:n], ACT.Copy).then_inc(ht_copied[1], 1)
                relu(k, slot, range(0, CT // 2))
                if not (isinstance(k, int) and k == STEPS - 1):
                    if chunk_of(k, LAG_STATS):
                        act.wait_ge(var_ready, k + 1)
                    if chunk_of(k, LAG_PQ):
                        act.wait_ge(var2_ready, k - LAG_PQ + 1)
                    nc.scalar.activation(rs[:, slot, 1, :], rs[:, slot, 0, :], ACT.Sqrt).then_inc(sd_ready, 1)
                relu(k, slot, range(CT // 2, CT))
            act.sem_inc(p_scaled, 2)
            over_steps(act, step)

        def nodes_vector(dve, early_weights, late_weights):
            def destinations():
                dve.wait_ge(idx_in, 16)
                nc.vector.tensor_copy(dst_f[:, :], dst_i[:, :]).then_inc(idx_done, 1)
                nc.vector.tensor_copy(base[:, :], dst_i[0:1, ::GT]).then_inc(idx_done, 1)

            def step(k, slot):
                if not (isinstance(k, int) and k == 0):
                    v, sd, r, t, res = (rs[:, 1 - slot, n, :] for n in range(5))
                    dve.wait_ge(sd_ready, k)
                    if not isinstance(k, int) or k >= 3:
                        dve.wait_ge(h_ready, min(k - 2, CHUNKS) if isinstance(k, int) else k - 2)
                    if not isinstance(k, int) or k >= LAG_SCALE + 2:
                        dve.wait_ge(p_scaled, k - LAG_SCALE + 1)
                    nc.vector.reciprocal(r, sd).then_inc(r_step, 1)
                    dve.wait_ge(r_step, 4 * k - 3)
                    nc.vector.tensor_tensor(t, r, r, ALU.mult).then_inc(r_step, 1)
                    dve.wait_ge(r_step, 4 * k - 2)
                    nc.vector.scalar_tensor_tensor(t, t, -0.5, v, ALU.mult, ALU.mult).then_inc(r_step, 1)
                    dve.wait_ge(r_step, 4 * k - 1)
                    nc.vector.scalar_tensor_tensor(res, t, 1.5, r, ALU.add, ALU.mult).then_inc(r_step, 1)
                    dve.wait_ge(r_step, 4 * k)
                if chunk_of(k, LAG_RELU):
                    c, tiles, rows = chunk_of(k, LAG_RELU)
                    nc.vector.scalar_tensor_tensor(
                        rs[0:rows, 1 - slot, 5, 0:tiles], mv[0:rows, 1 - slot, 0:tiles, 0], -1.0,
                        rs[0:rows, 1 - slot, 4, 0:tiles], ALU.mult, ALU.mult).then_inc(norm_ready, 1)
                if chunk_of(k, LAG_SCALE):
                    c, tiles, rows = chunk_of(k, LAG_SCALE)
                    dve.wait_ge(q_out[1 - slot], slot_loaded(c, 1 - slot))
                    for t in range(tiles):
                        ins = nc.vector.scalar_tensor_tensor(
                            pq_s[0:rows, 1 - slot, t, FEAT:2 * FEAT], pq_ps[0:rows, 1 - slot, 1, t, :],
                            rs[0:rows, 1 - slot, 4, CT + t:CT + t + 1], q_bias[0:rows, :], ALU.mult, ALU.add)
                    ins.then_inc(q_scaled, 1)
                if chunk_of(k, LAG_STATS):
                    c, tiles, rows = chunk_of(k, LAG_STATS)
                    dve.wait_ge(x_in[slot], slot_loaded(c, slot))
                    for t in range(tiles):
                        xt = x_s[0:rows, bass.ds(c * CT + t, 1), :].rearrange("p a h -> p (a h)")
                        ins = nc.vector.bn_stats(bn6[0:rows, slot, t, :], xt)
                    ins.then_inc(bn_step, 1)
                    dve.wait_ge(bn_step, 2 * c + 1)
                    dve.sem_inc(aggr_turn, 1)
                    for t in range(tiles):
                        ins = nc.vector.bn_aggr(mv[0:rows, slot, t, :], bn6[0:rows, slot, t, :])
                    ins.then_inc(bn_step, 1)
                    dve.wait_ge(bn_step, 2 * c + 2)
                    nc.vector.tensor_scalar(rs[0:rows, slot, 0, 0:tiles], mv[0:rows, slot, 0:tiles, 1], EPS, None,
                                            ALU.add).then_inc(var_ready, 1)
                if chunk_of(k, LAG_TRANSPOSE):
                    c, tiles, rows = chunk_of(k, LAG_TRANSPOSE)
                    n = (tiles - 1) * P + rows
                    dve.wait_ge(ht_ready, c + 1)
                    if reused(c):
                        dve.wait_ge(y_ready, c - 1)
                    nc.vector.tensor_copy(ht_s[:, slot, 0, 0:n], ht_ps[:, 0, 0:n]).then_inc(ht_copied[0], 1)
                if chunk_of(k, LAG_PQ):
                    c, tiles, rows = chunk_of(k, LAG_PQ)
                    dve.wait_ge(pq_ready, c + 1)
                    nc.vector.tensor_scalar(rs[0:rows, slot, 0, CT:CT + tiles], ss_ps[0:rows, 0:tiles],
                                            1.0 / FEAT, EPS, ALU.mult, ALU.add).then_inc(var2_ready, 1)
                if is_step(k, 0):
                    early_weights()
                if is_step(k, 2):
                    late_weights()
                if is_step(k, LAG_TRANSPOSE + CHUNKS - 1):
                    destinations()

            def relative():
                dve.wait_ge(idx_mm, 1)
                dve.wait_ge(idx_done, 1)
                nc.vector.tensor_tensor(rel[:, :].rearrange("p (g t) -> p g t", t=GT),
                                        dst_f[:, :].rearrange("p (g t) -> p g t", t=GT),
                                        base_ps.unsqueeze(2).to_broadcast([P, GROUPS, GT]),
                                        ALU.subtract).then_inc(idx_done, 1)
                dve.wait_ge(idx_done, 3)
                nc.vector.tensor_scalar(miss[:, :], rel[:, :], 0.0, None, ALU.is_lt).then_inc(idx_done, 1)
                dve.wait_ge(idx_done, 4)
                nc.vector.scalar_tensor_tensor(miss[:, :], rel[:, :], float(WIN), miss[:, :], ALU.is_ge, ALU.add,
                                               accum_out=miss_n[:, 0:1]).then_inc(idx_done, 1)

            dve.sem_inc(q_scaled, 2)
            over_steps(dve, step)
            relative()
            dve.wait_ge(idx_mm, 2)
            nc.vector.tensor_copy(miss_i[:, :], miss_ps[:, 0:1]).then_inc(idx_done, 1)

        with nc.Block() as block:
            @block.sync
            def _(sp):
                def load_x(c):
                    if c >= 2:
                        sp.wait_ge(x_in[c % 2], 16 * (c // 2))
                    if c < FULL_CHUNKS:
                        sp.dma_start(x_s[:, c * CT:(c + 1) * CT, :],
                                     x[c * CHUNK:(c + 1) * CHUNK, :].rearrange("(t p) h -> p t h", p=P))\
                          .then_inc(x_in[c % 2], 16)
                    else:
                        sp.dma_start(x_s[0:LAST_ROWS, c * CT, :], x[c * CHUNK:NODES, :]).then_inc(x_in[c % 2], 16)
                sp.dma_start(ntm_s[:, :], ntm_w).then_inc(w_in, 16)
                load_x(0)
                sp.dma_start(l1_s[:, :], l1_w).then_inc(w_in, 16)
                sp.dma_start(l2_s[:, :], l2_w).then_inc(late_w_in, 16)
                sp.dma_start(mtn_s[:, :, :], mtn_w.rearrange("(a p) f -> p a f", p=P)).then_inc(late_w_in, 16)
                sp.wait_ge(masks, N_MASKS)
                sp.dma_start(rtm_s[:, RBF_ROW:P], rtm_w).then_inc(late_w_in, 16)
                for slot in range(2):
                    sp.sem_inc(p_out[slot], 16)
                    sp.sem_inc(q_out[slot], 16)
                for c in range(1, CHUNKS):
                    load_x(c)
                sp.dma_start(dst_i[:, :], dst).then_inc(idx_in, 16)
                sp.wait_ge(acc_zero, 1)
                pad_rows = TABLE_ROWS - NODES
                sp.dma_start(q_table[NODES:TABLE_ROWS, :].rearrange("(a b) f -> a (b f)", b=3),
                             acc[0:pad_rows // 3, 0:3 * FEAT]).then_inc(zero_out, 16)

                def store(c, slot, tiles, rows):
                    for k, (table, scaled, done) in enumerate(((p_table, p_scaled, p_out),
                                                               (q_table, q_scaled, q_out))):
                        sp.wait_ge(scaled, c + 3)
                        part = slice(k * FEAT, (k + 1) * FEAT)
                        if tiles == CT:
                            sp.dma_start(table[bass.ds(c * CHUNK, CHUNK), :].rearrange("(t p) f -> p t f", p=P),
                                         pq_s[:, slot, :, part]).then_inc(done[slot], 16)
                        else:
                            sp.dma_start(table[c * CHUNK:NODES, :], pq_s[0:rows, slot, 0, part])\
                              .then_inc(done[slot], 16)
                over_chunks(sp, store)
                sp.wait_ge(zero_out, 16)
                for slot in range(2):
                    sp.wait_ge(q_out[slot], stored(last_of(slot), slot))
                sp.wait_ge(idx_done, 2)
                sp.wait_ge(consts, N_CONSTS)
                sp.wait_ge(w_done, N_WEIGHTS)
                pass_sync(sp)
                missed_passes(sp, pass_sync)
                result_sync(sp)

            @block.gpsimd
            def _(pool):
                def then_mask(ins):
                    ins.then_inc(masks, 1)

                def then_const(ins):
                    ins.then_inc(consts, 1)
                then_mask(nc.gpsimd.memset(center[:, :], -1.0 / FEAT))
                then_mask(nc.gpsimd.memset(ident[:, :], 0.0))
                then_mask(nc.gpsimd.memset(ones[:, :], 1.0))
                pool.wait_ge(masks, 3)
                nc.gpsimd.affine_select(out=center[:, :], in_=center[:, :], compare_op=ALU.not_equal,
                                        fill=1.0 - 1.0 / FEAT, base=0, pattern=[[-1, P]],
                                        channel_multiplier=1).then_inc(eye_ready, 1)
                nc.gpsimd.affine_select(out=ident[:, :], in_=ident[:, :], compare_op=ALU.not_equal,
                                        fill=1.0, base=0, pattern=[[-1, P]], channel_multiplier=1)\
                  .then_inc(eye_ready, 1)
                then_mask(nc.gpsimd.memset(rtm_s[:, :], 0.0))
                then_const(nc.gpsimd.memset(ones_bf[:, :], 1.0))
                then_const(nc.gpsimd.iota(iota[:, :], [[1, WIN]], base=0, channel_multiplier=0,
                                          allow_small_or_imprecise_dtypes=True))
                pool.wait_ge(eye_ready, 2)
                then_const(nc.gpsimd.tensor_copy(ident_bf[:, :], ident[:, :]))
                then_const(nc.gpsimd.memset(edge_t[:, :, :], 0.0))
                nc.gpsimd.memset(acc[:, :], 0.0).then_inc(acc_zero, 1)
                for slot in range(2):
                    pool.wait_ge(p_out[slot], stored(last_of(slot), slot))
                pass_gpsimd(pool)
                missed_passes(pool, pass_gpsimd, reset_gathers)

            @block.tensor
            def _(pe):
                pe.wait_ge(masks, N_MASKS)
                pe.wait_ge(eye_ready, 2)
                pe.wait_ge(w_in, 16 * 2)
                for n in range(2):
                    ins = nc.tensor.matmul(ntm_ps[:, n * P:(n + 1) * P], ntm_s[:, n * P:(n + 1) * P],
                                           center[:, :], start=True, stop=True)
                ins.then_inc(w_mm, 1)
                for n in range(3):
                    ins = nc.tensor.matmul(l1_ps[:, n * P:(n + 1) * P], l1_s[:, n * P:(n + 1) * P],
                                           center[:, :], start=True, stop=True)
                ins.then_inc(w_mm, 1)
                pe.wait_ge(cols_in, 16 * 6)
                nc.tensor.matmul(ntm_b_ps, center[:, :], cols[:, 0:1], start=True, stop=True).then_inc(w_mm, 1)
                pe.wait_ge(late_w_in, 16 * 3)
                for n, w in enumerate((mtn_s[:, 0, :], mtn_s[:, 1, :], l2_s[:, :])):
                    ins = nc.tensor.transpose(ml_ps[:, n * P:(n + 1) * P], w, ident[:, :])
                ins.then_inc(w_mm, 1)
                pe.wait_ge(w_done, 7)
                for n, (lhs, rhs) in enumerate(((vec_rep[:, 0, :], l1_t[:, 0, :]), (vec_rep[:, 0, :], l1_t[:, 1, :]),
                                                (vec_rep[:, 1, :], l1_t[:, 2, :]), (vec_rep[:, 2, :], center[:, :]))):
                    nc.tensor.matmul(bias_ps, lhs, rhs, start=(n == 0), stop=(n == 3))
                nc.tensor.matmul(wr_ps, rtm_s[:, :], l1_t[:, 2, :], start=True, stop=True).then_inc(w_mm, 1)
                nodes_tensor(pe)
                pe.wait_ge(p_scaled, CHUNKS + 2)
                pe.wait_ge(q_scaled, CHUNKS + 2)
                pe.wait_ge(idx_done, N_IDX)
                pe.wait_ge(consts, N_CONSTS)
                pass_tensor(pe)
                missed_passes(pe, pass_tensor)
                result_tensor(pe)

            @block.scalar
            def _(act):
                for k, v in enumerate((ntm_b, norm_b, rtm_b, l1_b, norm_g, l2_b)):
                    act.dma_start(cols[:, k:k + 1], v.rearrange("(f a) -> f a", a=1)).then_inc(cols_in, 16)
                act.dma_start(lng_b[:, :], ln_g.rearrange("(a f) -> a f", a=1).to_broadcast([P, FEAT]))\
                   .then_inc(bc_in, 16)
                act.dma_start(lnb_b[:, :], ln_b.rearrange("(a f) -> a f", a=1).to_broadcast([P, FEAT]))\
                   .then_inc(bc_in, 16)
                nodes_scalar(act)
                act.wait_ge(consts, N_CONSTS)
                pass_scalar(act)
                missed_passes(act, pass_scalar)
                result_scalar(act)

            @block.vector
            def _(dve):
                def copied(ins):
                    ins.then_inc(w_done, 1)
                def early_weights():
                    dve.wait_ge(w_mm, 1)
                    copied(nc.vector.tensor_copy(ntm_t[:, :, :].rearrange("p a f -> p (a f)"), ntm_ps))
                    dve.wait_ge(w_mm, 2)
                    copied(nc.vector.tensor_copy(l1_t[:, :, :].rearrange("p a f -> p (a f)"), l1_ps))
                    dve.wait_ge(cols_in, 16 * 6)
                    for k in range(3):
                        copied(nc.vector.tensor_scalar(vec_rep[:, k, :], ones[:, :], cols[:, 1 + k:2 + k], None,
                                                       ALU.mult))
                    dve.wait_ge(w_done, 2)
                    for k in range(2):
                        copied(nc.vector.tensor_scalar(ab_t[:, k * FEAT:(k + 1) * FEAT], l1_t[:, k, :],
                                                       cols[:, 4:5], None, ALU.mult))
                    dve.wait_ge(w_mm, 3)
                    copied(nc.vector.tensor_copy(ntm_bc[:, :], ntm_b_ps))
                    copied(nc.vector.memset(win_q[64:P, :, :], 0.0))

                def late_weights():
                    dve.wait_ge(w_mm, 4)
                    copied(nc.vector.tensor_copy(ml_t[:, :], ml_ps))
                    dve.wait_ge(w_mm, 5)
                    dve.wait_ge(w_done, EARLY_WEIGHTS)
                    for s in range(2):
                        copied(nc.vector.tensor_copy(win_q[RBF_ROW:P, s, :], wr_ps[RBF_ROW:P, :]))
                    copied(nc.vector.tensor_copy(q_bias[:, :], bias_ps))

                nc.vector.memset(rs[:, :, 0, :], 1.0).then_inc(rs_set, 1)
                dve.wait_ge(rs_set, 1)
                nodes_vector(dve, early_weights, late_weights)
                dve.wait_ge(bc_in, 16 * 2)
                dve.wait_ge(consts, N_CONSTS)
                dve.wait_ge(acc_zero, 1)
                pass_vector(dve)
                missed_passes_vector(dve)
                result_vector(dve)


def kernel(x, src, dst, edge_attr_32, L0_gnn_ntm_w, L0_gnn_ntm_b, L0_gnn_rtm_w, L0_gnn_rtm_b,
           L0_gnn_norm_g, L0_gnn_norm_b, L0_gnn_l1_w, L0_gnn_l1_b, L0_gnn_ln_g, L0_gnn_ln_b,
           L0_gnn_l2_w, L0_gnn_l2_b, L0_gnn_mtn_w):
    import numpy as np
    import concourse.bacc as bacc
    from concourse.bass_utils import run_bass_kernel_spmd

    def tiles_of(index, filler):
        padded = np.full(PAD_EDGES, filler, np.int32)
        padded[:EDGES] = index
        return np.ascontiguousarray(padded.reshape(EDGE_TILES, P).T)

    src_t = tiles_of(np.asarray(src), 0).reshape(P, PAIRS, 2 * GT).transpose(1, 0, 2)
    rbf_t = np.zeros((RBF, PAD_EDGES), np.float32)
    rbf_t[:, :EDGES] = np.asarray(edge_attr_32).T
    arrays = {
        "x": x, "src": src_t, "dst": tiles_of(np.asarray(dst), NODES), "rbf_t": rbf_t,
        "ntm_w": L0_gnn_ntm_w, "ntm_b": L0_gnn_ntm_b, "rtm_w": L0_gnn_rtm_w, "rtm_b": L0_gnn_rtm_b,
        "norm_g": L0_gnn_norm_g, "norm_b": L0_gnn_norm_b, "l1_w": L0_gnn_l1_w, "l1_b": L0_gnn_l1_b,
        "ln_g": L0_gnn_ln_g, "ln_b": L0_gnn_ln_b, "l2_w": L0_gnn_l2_w, "l2_b": L0_gnn_l2_b,
        "mtn_w": L0_gnn_mtn_w,
    }
    arrays = {f"in_{k}": np.ascontiguousarray(v) for k, v in arrays.items()}
    nc = bacc.Bacc("TRN2", target_bir_lowering=False, num_devices=1)
    args = [nc.dram_tensor(k, a.shape, mybir.dt.from_np(a.dtype), kind="ExternalInput").ap()
            for k, a in arrays.items()]
    out = nc.dram_tensor("out", (NODES, HID), F32, kind="ExternalOutput").ap()
    bass_gnn_layer(nc, *args, out)
    result = run_bass_kernel_spmd(nc, [arrays], core_ids=[0])
    return result.results[0]["out"]
```
